# Optimizing a Trainium2 kernel written in Bass

```python
import numpy as np
import jax
import jax.numpy as jnp

def _softmax(x, axis=-1):
    return jax.nn.softmax(x, axis=axis)

def _gelu(x):
    return jax.nn.gelu(x, approximate=True)

def _silu(x):
    return jax.nn.silu(x)

def _sigmoid(x):
    return jax.nn.sigmoid(x)

def _layernorm(x, axis=-1, eps=1e-05):
    m = jnp.mean(x, axis=axis, keepdims=True)
    v = jnp.var(x, axis=axis, keepdims=True)
    return (x - m) / jnp.sqrt(v + eps)

def _scatter_add(tgt, idx, src, axis=0):
    return tgt.at[idx].add(src)

def _segment_sum(src, seg, n):
    return jax.ops.segment_sum(src, seg, n)
kernel_name = 'mk_flamingo_gated_d2_seqx_r8_2837df'

def setup_inputs(seed: int=0):
    np.random.seed(seed)
    _w = jnp.asarray

    def _rec_inputs():
        import jax
        import jax.numpy as jnp
        _rk = jax.random.key(seed)
        x = 7.22e-05 + 1 * jax.random.normal(jax.random.fold_in(_rk, 1), (16, 256, 128), jnp.float32)
        _lenS = 256 - jax.random.randint(jax.random.fold_in(_rk, 7), (16,), 0, max(1, 256 // 4) + 1, jnp.int32)
        _lenS2 = 1601 - jax.random.randint(jax.random.fold_in(_rk, 8), (16,), 0, max(1, 1601 // 4) + 1, jnp.int32)
        _ctx_1024P = jax.random.normal(jax.random.fold_in(_rk, 11), (16, 16, 128), jnp.float32)
        _ctx_1024c = jax.random.dirichlet(jax.random.fold_in(_rk, 511), 0.3 * jnp.ones((16,), jnp.float32), (16, 1601))
        _ctx_1024t = jnp.einsum('bsk,bkd->bsd', _ctx_1024c, _ctx_1024P)
        _ctx_1024t = _ctx_1024t * jax.lax.rsqrt(jnp.mean(jnp.square(_ctx_1024t)) + 1e-12) * 0.953939
        ctx_1024 = 4.13588e-05 + 0.999923 * (_ctx_1024t + 0.3 * jax.random.normal(jax.random.fold_in(_rk, 611), (16, 1601, 128), jnp.float32))
        _g = jax.random.normal(jax.random.fold_in(_rk, 9001), (2, 2), jnp.float32)
        _g = jnp.sign(_g) * jnp.maximum(jnp.abs(_g), 1.0) + (_g == 0) * 1.0
        g_xattn = _g[0]
        g_ffn = _g[1]
        return (x, ctx_1024, g_xattn, g_ffn)
    x, ctx_1024, g_xattn, g_ffn = _rec_inputs()

    def _L0_xattn_setup():
        import jax, jax.numpy as jnp
        import numpy as np
        D_MODEL = 128
        NUM_HEADS = 16
        D_K = D_MODEL // NUM_HEADS

        def _split_heads(x):
            B, S, _ = x.shape
            return x.reshape(B, S, NUM_HEADS, D_K).transpose(0, 2, 1, 3)
        key = jax.random.key(seed)
        ks = jax.random.split(key, 11)
        B, S = (4, 256)
        s = 1.0 / np.sqrt(D_MODEL)
        return {'query': jax.random.normal(ks[0], (B, S, D_MODEL), jnp.float32), 'key': jax.random.normal(ks[1], (B, S, D_MODEL), jnp.float32), 'value': jax.random.normal(ks[2], (B, S, D_MODEL), jnp.float32), 'Wq': jax.random.normal(ks[3], (D_MODEL, D_MODEL), jnp.float32) * s, 'bq': jnp.zeros((D_MODEL,), jnp.float32), 'Wk': jax.random.normal(ks[4], (D_MODEL, D_MODEL), jnp.float32) * s, 'bk': jnp.zeros((D_MODEL,), jnp.float32), 'Wv': jax.random.normal(ks[5], (D_MODEL, D_MODEL), jnp.float32) * s, 'bv': jnp.zeros((D_MODEL,), jnp.float32), 'Wo': jax.random.normal(ks[6], (D_MODEL, D_MODEL), jnp.float32) * s, 'bo': jnp.zeros((D_MODEL,), jnp.float32)}
    _L0_xattn_all = _L0_xattn_setup()
    _L0_xattn_in = {k: v for k, v in _L0_xattn_all.items() if k in ('Wq', 'bq', 'Wk', 'bk', 'Wv', 'bv', 'Wo', 'bo')}
    del _L0_xattn_all

    def _L0_ffn_setup():
        import jax, jax.numpy as jnp
        import numpy as np
        E = 8
        K = 2
        D = 128
        P = 512
        key = jax.random.key(seed)
        ks = jax.random.split(key, 8)
        s = lambda fan_in: 1.0 / np.sqrt(fan_in)
        x = jax.random.normal(ks[0], (2, 256, D), dtype=jnp.float32)
        W1 = jax.random.normal(ks[1], (E, D, P), dtype=jnp.float32) * s(D)
        b1 = jax.random.normal(ks[2], (E, P), dtype=jnp.float32) * 0.01
        W2 = jax.random.normal(ks[3], (E, P, D), dtype=jnp.float32) * s(P)
        b2 = jax.random.normal(ks[4], (E, D), dtype=jnp.float32) * 0.01
        Wr = jax.random.normal(ks[5], (D, E), dtype=jnp.float32) * s(D)
        br = jax.random.normal(ks[6], (E,), dtype=jnp.float32) * 0.01
        return {'x': x, 'W1': W1, 'b1': b1, 'W2': W2, 'b2': b2, 'Wr': Wr, 'br': br}
    _L0_ffn_all = _L0_ffn_setup()
    _L0_ffn_in = {k: v for k, v in _L0_ffn_all.items() if k in ('W1', 'b1', 'W2', 'b2', 'Wr', 'br')}
    del _L0_ffn_all

    def _L1_xattn_setup():
        import jax, jax.numpy as jnp
        import numpy as np
        HID, NH, TOPK = (128, 16, 32)
        HD = HID // NH
        SCALE = float(np.sqrt(HD))

        def _split_heads(x, B, L):
            return x.reshape(B, L, NH, HD).transpose(0, 2, 1, 3)
        key = jax.random.key(seed)
        ks = jax.random.split(key, 12)
        B, Q, KV = (2, 256, 512)
        s = 0.02
        return {'query': jax.random.normal(ks[0], (B, Q, HID), jnp.float32), 'key': jax.random.normal(ks[1], (B, KV, HID), jnp.float32), 'value': jax.random.normal(ks[2], (B, KV, HID), jnp.float32), 'Wq': jax.random.normal(ks[3], (HID, HID), jnp.float32) * s, 'bq': jnp.zeros((HID,), jnp.float32), 'Wk': jax.random.normal(ks[4], (HID, HID), jnp.float32) * s, 'bk': jnp.zeros((HID,), jnp.float32), 'Wv': jax.random.normal(ks[5], (HID, HID), jnp.float32) * s, 'bv': jnp.zeros((HID,), jnp.float32), 'Wo': jax.random.normal(ks[6], (HID, HID), jnp.float32) * s, 'bo': jnp.zeros((HID,), jnp.float32)}
    _L1_xattn_all = _L1_xattn_setup()
    _L1_xattn_in = {k: v for k, v in _L1_xattn_all.items() if k in ('Wq', 'bq', 'Wk', 'bk', 'Wv', 'bv', 'Wo', 'bo')}
    del _L1_xattn_all

    def _L1_ffn_setup():
        import jax, jax.numpy as jnp
        import numpy as np
        NUM_HEADS = 16
        TOP_K = 2
        key = jax.random.key(seed)
        ks = jax.random.split(key, 5)
        B, S, D, E = (4, 256, 128, 8)
        scale = 0.02
        return {'x': jax.random.normal(ks[0], (B, S, D), dtype=jnp.float32), 'W_qkv': jax.random.normal(ks[1], (D, 3 * D), dtype=jnp.float32) * scale, 'b_qkv': jnp.zeros((3 * D,), dtype=jnp.float32), 'W_gate': jax.random.normal(ks[2], (D, E), dtype=jnp.float32) * scale, 'b_gate': jnp.zeros((E,), dtype=jnp.float32), 'W_experts': jax.random.normal(ks[3], (E, D, D), dtype=jnp.float32) * scale, 'b_experts': jnp.zeros((E, D), dtype=jnp.float32)}
    _L1_ffn_all = _L1_ffn_setup()
    _L1_ffn_in = {k: v for k, v in _L1_ffn_all.items() if k in ('W_qkv', 'b_qkv', 'W_gate', 'b_gate', 'W_experts', 'b_experts')}
    del _L1_ffn_all
    return {'x': x, 'ctx_1024': ctx_1024, 'g_xattn': g_xattn, 'g_ffn': g_ffn, 'L0_xattn_Wq': _L0_xattn_in['Wq'], 'L0_xattn_bq': _L0_xattn_in['bq'], 'L0_xattn_Wk': _L0_xattn_in['Wk'], 'L0_xattn_bk': _L0_xattn_in['bk'], 'L0_xattn_Wv': _L0_xattn_in['Wv'], 'L0_xattn_bv': _L0_xattn_in['bv'], 'L0_xattn_Wo': _L0_xattn_in['Wo'], 'L0_xattn_bo': _L0_xattn_in['bo'], 'L0_ffn_W1': _L0_ffn_in['W1'], 'L0_ffn_b1': _L0_ffn_in['b1'], 'L0_ffn_W2': _L0_ffn_in['W2'], 'L0_ffn_b2': _L0_ffn_in['b2'], 'L0_ffn_Wr': _L0_ffn_in['Wr'], 'L0_ffn_br': _L0_ffn_in['br'], 'L1_xattn_Wq': _L1_xattn_in['Wq'], 'L1_xattn_bq': _L1_xattn_in['bq'], 'L1_xattn_Wk': _L1_xattn_in['Wk'], 'L1_xattn_bk': _L1_xattn_in['bk'], 'L1_xattn_Wv': _L1_xattn_in['Wv'], 'L1_xattn_bv': _L1_xattn_in['bv'], 'L1_xattn_Wo': _L1_xattn_in['Wo'], 'L1_xattn_bo': _L1_xattn_in['bo'], 'L1_ffn_W_qkv': _L1_ffn_in['W_qkv'], 'L1_ffn_b_qkv': _L1_ffn_in['b_qkv'], 'L1_ffn_W_gate': _L1_ffn_in['W_gate'], 'L1_ffn_b_gate': _L1_ffn_in['b_gate'], 'L1_ffn_W_experts': _L1_ffn_in['W_experts'], 'L1_ffn_b_experts': _L1_ffn_in['b_experts']}

def reference(x, ctx_1024, g_xattn, g_ffn, L0_xattn_Wq, L0_xattn_bq, L0_xattn_Wk, L0_xattn_bk, L0_xattn_Wv, L0_xattn_bv, L0_xattn_Wo, L0_xattn_bo, L0_ffn_W1, L0_ffn_b1, L0_ffn_W2, L0_ffn_b2, L0_ffn_Wr, L0_ffn_br, L1_xattn_Wq, L1_xattn_bq, L1_xattn_Wk, L1_xattn_bk, L1_xattn_Wv, L1_xattn_bv, L1_xattn_Wo, L1_xattn_bo, L1_ffn_W_qkv, L1_ffn_b_qkv, L1_ffn_W_gate, L1_ffn_b_gate, L1_ffn_W_experts, L1_ffn_b_experts):
    import jax
    import jax.numpy as jnp

    def _L0_xattn_ref(query, key, value, Wq, bq, Wk, bk, Wv, bv, Wo, bo):
        import jax, jax.numpy as jnp
        import numpy as np
        D_MODEL = 128
        NUM_HEADS = 16
        D_K = D_MODEL // NUM_HEADS

        def _split_heads(x):
            B, S, _ = x.shape
            return x.reshape(B, S, NUM_HEADS, D_K).transpose(0, 2, 1, 3)
        B, Sq, _ = query.shape
        q = _split_heads(query @ Wq.T + bq)
        k = _split_heads(key @ Wk.T + bk)
        v = _split_heads(value @ Wv.T + bv)
        scores = jnp.einsum('bhqd,bhkd->bhqk', q, k) / jnp.sqrt(jnp.float32(D_K))
        attn = jax.nn.softmax(scores, axis=-1)
        ctx = jnp.einsum('bhqk,bhkd->bhqd', attn, v)
        ctx = ctx.transpose(0, 2, 1, 3).reshape(B, Sq, D_MODEL)
        return ctx @ Wo.T + bo

    def _L0_ffn_ref(x, W1, b1, W2, b2, Wr, br):
        import jax, jax.numpy as jnp
        import numpy as np
        E = 8
        K = 2
        D = 128
        P = 512
        B, S, _ = x.shape
        xf = x.reshape(B * S, D)
        scores = xf @ Wr + br
        _, top_idx = jax.lax.top_k(scores, K)
        mask = jax.nn.one_hot(top_idx, E, dtype=scores.dtype).sum(-2) > 0
        router_weights = jax.nn.softmax(jnp.where(mask, scores, -jnp.inf), axis=-1)
        h = jax.nn.gelu(jnp.einsum('td,edp->etp', xf, W1) + b1[:, None, :])
        y = jnp.einsum('etp,epd->etd', h, W2) + b2[:, None, :]
        out = jnp.einsum('te,etd->td', router_weights, y)
        return out.reshape(B, S, D)

    def _L1_xattn_ref(query, key, value, Wq, bq, Wk, bk, Wv, bv, Wo, bo):
        import jax, jax.numpy as jnp
        import numpy as np
        HID, NH, TOPK = (128, 16, 32)
        HD = HID // NH
        SCALE = float(np.sqrt(HD))

        def _split_heads(x, B, L):
            return x.reshape(B, L, NH, HD).transpose(0, 2, 1, 3)
        B, Q, _ = query.shape
        KV = key.shape[1]
        q = _split_heads(query @ Wq.T + bq, B, Q)
        k = _split_heads(key @ Wk.T + bk, B, KV)
        v = _split_heads(value @ Wv.T + bv, B, KV)
        scores = jnp.einsum('bhqd,bhkd->bhqk', q, k) / SCALE
        eff_k = min(TOPK, KV)
        top_scores, top_idx = jax.lax.top_k(scores, eff_k)
        w = jax.nn.softmax(top_scores, axis=-1)
        top_v = jnp.take_along_axis(v[:, :, None, :, :], top_idx[..., None], axis=3)
        out = jnp.einsum('bhqk,bhqkd->bhqd', w, top_v)
        out = out.transpose(0, 2, 1, 3).reshape(B, Q, HID)
        return out @ Wo.T + bo

    def _L1_ffn_ref(x, W_qkv, b_qkv, W_gate, b_gate, W_experts, b_experts):
        import jax, jax.numpy as jnp
        import numpy as np
        NUM_HEADS = 16
        TOP_K = 2
        B, S, D = x.shape
        H = NUM_HEADS
        hd = D // H
        E = W_gate.shape[-1]
        qkv = (x @ W_qkv + b_qkv).reshape(B, S, 3, H, hd)
        q, k, v = (qkv[:, :, 0], qkv[:, :, 1], qkv[:, :, 2])
        attn = jnp.einsum('bqhd,bkhd->bhqk', q, k) / jnp.sqrt(jnp.asarray(hd, x.dtype))
        attn = jax.nn.softmax(attn, axis=-1)
        attn_out = jnp.einsum('bhqk,bkhd->bqhd', attn, v).reshape(B, S, D)
        gate = jax.nn.softmax(x @ W_gate + b_gate, axis=-1)
        top_g, top_i = jax.lax.top_k(gate, TOP_K)
        combine = jnp.sum(jax.nn.one_hot(top_i, E, dtype=x.dtype) * top_g[..., None], axis=2)
        expert_out = jnp.einsum('bsd,edf->bsef', x, W_experts) + b_experts
        moe_out = jnp.einsum('bsef,bse->bsf', expert_out, combine)
        return attn_out + moe_out
    x = x + jnp.tanh(g_xattn[0]) * _L0_xattn_ref(_layernorm(x, axis=-1), ctx_1024, ctx_1024, L0_xattn_Wq, L0_xattn_bq, L0_xattn_Wk, L0_xattn_bk, L0_xattn_Wv, L0_xattn_bv, L0_xattn_Wo, L0_xattn_bo)
    x = x + jnp.tanh(g_ffn[0]) * _L0_ffn_ref(_layernorm(x, axis=-1), L0_ffn_W1, L0_ffn_b1, L0_ffn_W2, L0_ffn_b2, L0_ffn_Wr, L0_ffn_br)
    x = x + jnp.tanh(g_xattn[1]) * _L1_xattn_ref(_layernorm(x, axis=-1), ctx_1024, ctx_1024, L1_xattn_Wq, L1_xattn_bq, L1_xattn_Wk, L1_xattn_bk, L1_xattn_Wv, L1_xattn_bv, L1_xattn_Wo, L1_xattn_bo)
    x = x + jnp.tanh(g_ffn[1]) * _L1_ffn_ref(_layernorm(x, axis=-1), L1_ffn_W_qkv, L1_ffn_b_qkv, L1_ffn_W_gate, L1_ffn_b_gate, L1_ffn_W_experts, L1_ffn_b_experts)
    return x

_drawn_inputs = setup_inputs


def setup_inputs(seed=0):
    import zlib

    import numpy as np

    out = dict(_drawn_inputs(seed))
    spreads = {'g_ffn': (-1.0, 0.6),
     'L0_xattn_bq': (0.0, 0.1),
     'L0_xattn_bk': (0.0, 0.8),
     'L0_xattn_bv': (0.0, 0.1),
     'L0_xattn_bo': (0.0, 0.1),
     'L1_xattn_bq': (0.0, 0.481),
     'L1_xattn_bk': (0.0, 0.8),
     'L1_xattn_bv': (0.0, 0.501),
     'L1_xattn_bo': (0.0, 0.1),
     'L1_ffn_b_qkv': (0.0, 0.1),
     'L1_ffn_b_gate': (0.0, 0.315),
     'L1_ffn_b_experts': (0.0, 0.489)}
    factors = {'L0_ffn_b1': 8.0, 'L0_ffn_b2': 8.0}
    for name, (base, spread) in spreads.items():
        noise = np.random.default_rng([zlib.crc32(name.encode()), seed]).standard_normal(out[name].shape)
        drawn = base * np.exp(spread * noise) if base else spread * noise
        out[name] = jnp.asarray(drawn.astype(out[name].dtype))
    for name, factor in factors.items():
        out[name] = (out[name] * factor).astype(out[name].dtype)
    return out
```

```python
import numpy as np
import concourse.bass as bass
import concourse.mybir as mybir
from concourse.alu_op_type import AluOpType as ALU
from contextlib import ExitStack

F32 = mybir.dt.float32
BF16 = mybir.dt.bfloat16
U32 = mybir.dt.uint32
ACT = mybir.ActivationFunctionType
AX = mybir.AxisListType

B, S, D = 16, 256, 128
NK = 1601
H, HD = 16, 8
P = 128
QT = S // P
G, HG = 4, 4
E, FF = 8, 512
PT = FF // P
TOPK = 32
NC = -(-NK // P)
BANK = 512
SCALE = float(1.0 / np.sqrt(HD))
EPS = 1e-5
NEG = -3.0e38
STEEP = 2.0 ** 66
GUARD = 60.0 / SCALE
ROUND = 2.0 ** -21

KPART = (0, 0, 0, 1, 1, 2)
QPART = (0, 1, 2, 0, 1, 0)
NT = len(KPART)
ROWS = NT * HD
ROWX = ROWS + 3


W_STEP = 3
SCAN0, ATT0, ATT0_AT, V_AT, V_STEP, SCAN1, ATT1, Z_AT, Z_STEP, Z_WAIT = 1.9, 1, 0.4, 1, 5, 1.9, 1, 2, 1, 3


def chunk(n, c):
    return min(P, n - c * P)


class Pass:

    def __init__(self, nc, sems, dma_sems):
        self.eng = {"pe": nc.tensor, "act": nc.scalar, "dve": nc.vector, "pool": nc.gpsimd, "sp": nc.sync}
        self.sem = sems
        self.count = {k: 0 for k in sems}
        self.dma_sem, self.streams = list(dma_sems), {}
        self.seen, self.stages = {}, []

    def wait(self, name, tokens):
        for t in tokens:
            if isinstance(t, list):
                self.wait(name, t)
            elif t is not None and self.seen.get((name, t[0]), 0) < t[1]:
                self.seen[(name, t[0])] = t[1]
                self.eng[name].wait_ge(t[2], t[1])

    def op(self, name, fn, after=()):
        if name in ("dve", "pool") and self.count[name]:
            self.wait(name, [(name, self.count[name], self.sem[name])])
        self.wait(name, after)
        fn(self.eng[name]).then_inc(self.sem[name], 1)
        self.count[name] += 1
        return (name, self.count[name], self.sem[name])

    def dma(self, stream, copies, after=()):
        if stream not in self.streams:
            self.streams[stream] = [self.dma_sem[len(self.streams)], 0]
        s = self.streams[stream]
        self.wait("sp", after)
        for out, in_ in copies:
            self.eng["sp"].dma_start(out, in_).then_inc(s[0], 16)
            s[1] += 16
        return (stream, s[1], s[0])

    def stage(self, at, gen):
        self.stages.append((at, len(self.stages), gen))

    def run(self):
        while self.stages:
            self.stages.sort(key=lambda s: s[:2])
            at, n, gen = self.stages.pop(0)
            step = next(gen, None)
            if step is not None:
                self.stages.append((at + step, n, gen))
        for stream, (sem, total) in self.streams.items():
            self.wait("sp", [(stream, total, sem)])


class Ring:

    def __init__(self, bufs):
        self.bufs, self.n = bufs, 0
        self.free, self.held = [None] * len(bufs), [False] * len(bufs)

    def take(self):
        i = self.n % len(self.bufs)
        self.n += 1
        assert not self.held[i]
        self.held[i] = True
        return i, self.bufs[i], self.free[i]

    def ready(self, k):
        return not any(self.held[(self.n + j) % len(self.bufs)] for j in range(k))

    def release(self, i, *tokens):
        assert self.held[i]
        self.free[i], self.held[i] = list(tokens), False


class Stages:

    def __init__(self, p, m, d):
        self.p, self.m, self.d = p, m, d
        self.ring = {k: Ring(v) for k, v in m.rings.items()}

    def turn(self, src, dst, ready):
        p, m = self.p, self.m
        i, ps, free = self.ring["small"].take()

        def tr(e):
            for t in range(QT):
                r = e.transpose(ps[:, t * P:(t + 1) * P], src[:, t, :], m.ident[:, :])
            return r
        t0 = p.op("pe", tr, [ready, free])
        t1 = p.op("act", lambda e: e.activation(dst[:, :], ps[:, 0:S], ACT.Copy), [t0])
        self.ring["small"].release(i, t1)
        return t1

    def norm(self, z, ready):
        p, m = self.p, self.m

        def stats(e):
            for t in range(QT):
                r = e.bn_stats(z["stats"][:, t, :], z["x"][:, t, :])
            return r
        t0 = p.op("dve", stats, [ready])

        def aggr(e):
            for t in range(QT):
                r = e.bn_aggr(z["mv"][:, t, :], z["stats"][:, t, :])
            return r
        t0 = p.op("dve", aggr, [t0])
        t0 = p.op("dve", lambda e: e.tensor_scalar_add(z["rstd"][:, :], z["mv"][:, :, 1], EPS), [t0])
        t0 = p.op("pool", lambda e: e.tensor_tensor(z["rstd"][:, :], z["rstd"][:, :], m.half[:, :], ALU.pow), [t0])
        yield 1

        def scale(e):
            for t in range(QT):
                r = e.tensor_scalar(z["xn"][:, t, :], z["x"][:, t, :], z["mv"][:, t, 0:1], z["rstd"][:, t:t + 1],
                                    ALU.subtract, ALU.mult)
            return r
        t0 = p.op("dve", scale, [t0])
        yield 1
        z["xnT_ready"] = self.turn(z["xn"], z["xnT"], t0)

    def split(self, src, part, n, ready, free):
        p = self.p
        t = p.op("pool", lambda e: e.tensor_copy(part[:, 0, 0:n], src[:, 0:n]), [ready, free])
        t = p.op("pool", lambda e: e.tensor_tensor(src[:, 0:n], src[:, 0:n], part[:, 0, 0:n], ALU.subtract), [t])
        t = p.op("pool", lambda e: e.tensor_copy(part[:, 1, 0:n], src[:, 0:n]), [t])
        return p.op("pool", lambda e: e.tensor_tensor(part[:, 2, 0:n], src[:, 0:n], part[:, 1, 0:n], ALU.subtract), [t])

    def to_stack(self, w, rhs, bias, n, stack, parts, cols, ready):
        p = self.p
        i, ps, free = self.ring["wide"].take()
        t0 = p.op("pe", lambda e: e.matmul(ps[:, 0:n], w, rhs, start=True, stop=True), [ready, free])
        fi, (f, part), ffree = self.ring["split"].take()
        t1 = p.op("act", lambda e: e.activation(f[:, 0:n], ps[:, 0:n], ACT.Identity, bias=bias), [t0, ffree])
        self.ring["wide"].release(i, t1)
        t2 = self.split(f, part, n, t1, ffree)
        t3 = p.dma(f"split{fi}", [(stack[k, :, :, cols].rearrange("j h s -> h j s"), part[:, parts[k], 0:n])
                                  for k in range(NT)], [t2])
        self.ring["split"].release(fi, t3)
        return t3

    def shift_rows(self, z, src, i, g, rows, ready, name):
        p, m = self.p, self.m
        n, ps, free = self.ring["small"].take()
        t = p.op("pe", lambda e: e.transpose(ps[0:8, 0:P], src[:, :], m.ident[:, :]), [ready, free])
        z["src_free"] = t
        t = p.op("act", lambda e: e.activation(z["minus"][:, :], ps[0:8, 0:P], ACT.Copy, scale=-1.0), [t])
        self.ring["small"].release(n, t)
        t = p.op("pool", lambda e: e.tensor_copy(z["shift"][:, 0, :], z["minus"][:, :]), [t, z["sent"]])
        t = p.op("pool", lambda e: e.tensor_tensor(z["res"][:, :], z["minus"][:, :], z["shift"][:, 0, :], ALU.subtract), [t])
        t = p.op("pool", lambda e: e.tensor_copy(z["shift"][:, 1, :], z["res"][:, :]), [t])
        t = p.op("pool", lambda e: e.tensor_tensor(z["shift"][:, 2, :], z["res"][:, :], z["shift"][:, 1, :], ALU.subtract), [t])
        z["sent"] = p.dma(name, [(rows[i, k, g, :, :], z["shift"][:, k, :]) for k in range(3)], [t])
        return z["sent"]

    def stage_w(self, i):
        p, m, d, z = self.p, self.m, self.d, self.m.z["w"]
        x = p.dma("w_x", [(z["x"][:, :, :], d.x[i, :, :].rearrange("(t p) d -> p t d", p=P))])
        c = p.dma("w_ctx", [(m.ctxT[:, :], d.ctx[i, :, :])])
        yield 3
        yield from self.norm(z, x)
        yield 1
        self.to_stack(m.w_qT[:, 0, :], z["xnT"][:, :], m.b_q[:, 0:1], S, d.q_stack[0][i], QPART, slice(0, S), z["xnT_ready"])
        yield 1
        for l in range(2):
            for k in range(-(-NK // BANK)):
                a, w = k * BANK, min(BANK, NK - k * BANK)
                self.to_stack(m.w_kT[:, l, :], m.ctxT[:, a:a + w], m.b_k[:, l:l + 1], w, d.k_stack[l][i], KPART,
                              slice(a, a + w), c)
                yield W_STEP
                cs = range(4 * k, min(4 * k + 4, NC))
                n, ps, free = self.ring["wide"].take()

                def mm(e):
                    for q, cc in enumerate(cs):
                        kc = chunk(NK, cc)
                        r = e.matmul(ps[0:kc, q * D:(q + 1) * D], m.ctxT[:, cc * P:cc * P + kc], m.w_vT[:, l, :],
                                     start=True, stop=True)
                    return r
                t0 = p.op("pe", mm, [c, free])
                vi, vo, vfree = self.ring["v_out"].take()
                kc = chunk(NK, cs[-1])
                t1 = p.op("act", lambda e: e.activation(
                    vo[0:kc, 0:len(cs) * H, 0:HD], ps[0:kc, 0:len(cs) * D].rearrange("p (c j) -> p c j", j=HD),
                    ACT.Copy), [t0, vfree])
                self.ring["wide"].release(n, t1)
                t2 = p.dma(f"v_out{vi}", [(d.v[l][i, 0:kc, cs[0]:cs[-1] + 1, :],
                                           vo[0:kc, 0:len(cs) * H, :].rearrange("p (c h) j -> p c (h j)", h=H))], [t1])
                self.ring["v_out"].release(vi, t2)
                yield W_STEP

    def stage_scan(self, l, i, step):
        p, m, d, z = self.p, self.m, self.d, self.m.z["scan%d" % l]
        z["sent"] = z["src_free"] = None
        name = "scan%d" % l
        qring, kring = self.ring["q_" + name], self.ring["k_" + name]

        def load_q(g):
            n, q, free = qring.take()
            t = p.dma(f"q_{name}_{n}", [(q[0:ROWS, :, :], d.q_stack[l][i, :, :, g * HG:(g + 1) * HG, :]
                                         .rearrange("n j h s -> (n j) h s"))], [free])
            return n, q, t

        def load_k(h):
            n, k, free = kring.take()
            t = p.dma(f"k_{name}_{n}", [(k[0:ROWS, :], d.k_stack[l][i, :, :, h, :].rearrange("n j s -> (n j) s"))],
                      [free])
            return n, k, t
        qs, ks = [load_q(0)], [load_k(0), load_k(1)]
        yield 1
        for g in range(G):
            if g + 1 < G:
                qs.append(load_q(g + 1))
            qn, q, q_ready = qs.pop(0)
            for hh in range(HG):
                h = g * HG + hh
                kn, k, k_ready = ks.pop(0)
                for qt in range(QT):
                    n = hh * QT + qt
                    if l == 0:
                        for c in range(-(-NK // BANK)):
                            a, w = c * BANK, min(BANK, NK - c * BANK)
                            si, ps, free = self.ring["score"].take()
                            t0 = p.op("pe", lambda e: e.matmul(ps[:, 0:w], q[0:ROWS, hh, qt * P:(qt + 1) * P],
                                                               k[0:ROWS, a:a + w], start=True, stop=True),
                                      [q_ready, k_ready, free])
                            last = p.op("dve", lambda e: e.tensor_reduce(z["part"][:, n, c:c + 1], ps[:, 0:w], AX.X,
                                                                         ALU.max), [t0])
                            self.ring["score"].release(si, last)
                            yield step / 4
                    else:
                        bi, s, sfree = self.ring["s"].take()
                        for c in range(-(-NK // (2 * BANK))):
                            a, w = c * 2 * BANK, min(2 * BANK, NK - c * 2 * BANK)
                            si, ps, free = self.ring["wide"].take()

                            def mm(e):
                                for b in range(0, w, BANK):
                                    r = e.matmul(ps[:, b:min(b + BANK, w)], q[0:ROWS, hh, qt * P:(qt + 1) * P],
                                                 k[0:ROWS, a + b:a + min(b + BANK, w)], start=True, stop=True)
                                return r
                            t0 = p.op("pe", mm, [q_ready, k_ready, free])
                            last = p.op("act", lambda e: e.activation(s[:, a:a + w], ps[:, 0:w], ACT.Copy), [t0, sfree])
                            self.ring["wide"].release(si, last)
                        yield step / 2
                        t1 = self.kth(s, z, n, last)
                        self.ring["s"].release(bi, t1)
                        yield step / 2
                kring.release(kn, t0)
                if h + 2 < H:
                    ks.append(load_k(h + 2))
            qring.release(qn, t0)
            if l == 0:
                last = p.op("dve", lambda e: e.tensor_reduce(z["mx"][:, :], z["part"][:, :, :], AX.X, ALU.max),
                            [last, z["src_free"]])
                src = z["mx"]
            else:
                last = self.threshold(z, t1)
                src = z["th"]
            yield step / 2
            self.shift_rows(z, src, i, g, d.rows[l], last, name + "_rows")

    def kth(self, s, z, n, ready):
        p, m = self.p, self.m
        t = p.op("dve", lambda e: e.max(m.top[:, 0, :], s[:, :]), [ready])
        for r in range(1, TOPK // 8):
            src = s if r == 1 else m.cut
            t = p.op("dve", lambda e: e.match_replace(m.cut[:, :], m.top[:, r - 1, :], src[:, :], NEG), [t])
            t = p.op("dve", lambda e: e.max(m.top[:, r, :], m.cut[:, :]), [t])
        p.op("dve", lambda e: e.tensor_copy(z["mx"][:, n:n + 1], m.top[:, 0, 0:1]), [t])
        return p.op("dve", lambda e: e.tensor_copy(z["kth"][:, n:n + 1], m.top[:, TOPK // 8 - 1, 7:8]))

    def threshold(self, z, ready):
        p = self.p
        def stt(out, x, c, y, op):
            return lambda e: e.scalar_tensor_tensor(out[:, :], x[:, :], c, y[:, :], ALU.mult, op)
        t = p.op("dve", stt(z["th"], z["mx"], -1.0, z["mx"], ALU.max), [ready, z["src_free"]])
        t = p.op("dve", stt(z["th"], z["th"], -ROUND, z["kth"], ALU.add), [t])
        t = p.op("dve", stt(z["kth"], z["kth"], -1.0, z["kth"], ALU.max), [t])
        t = p.op("dve", stt(z["th"], z["kth"], -ROUND, z["th"], ALU.add), [t])
        return p.op("dve", lambda e: e.scalar_tensor_tensor(z["th"][:, :], z["mx"][:, :], -GUARD, z["th"][:, :],
                                                            ALU.add, ALU.max), [t])

    def weigh(self, g, nk, kq, v, topk, step, last_group, z):
        p, m = self.p, self.m
        pend = []
        while not self.ring["att"].ready(1):
            yield 0.25
        ai, ap, afree = self.ring["att"].take()

        def sums():
            c, kc, pi, pr, t2 = pend.pop(0)

            def mm(e):
                for j in range(HG):
                    r = e.matmul(ap[32 * j:32 * j + HD + 1, 0:S], v[0:kc, c, g * HG + j, :],
                                 pr[0:kc, j * S:(j + 1) * S], start=(c == 0), stop=(c * P + kc == nk),
                                 tile_position=(0, 32 * j), skip_group_check=True)
                return r
            t3 = p.op("pe", mm, [t2, afree if c == 0 else None])
            self.ring["prob"].release(pi, t3)
            return t3
        def scores(c):
            kc = chunk(nk, c)
            k, q, c0, ready, done = kq(c)
            i, ps, free = self.ring["wide"].take()

            def mm(e):
                for j in range(HG):
                    r = e.matmul(ps[0:kc, j * S:(j + 1) * S], k[0:ROWX, j, c0:c0 + kc], q[0:ROWX, j, :],
                                 start=(j % 2 == 0), stop=not topk, skip_group_check=True)
                return r
            t = p.op("pe", mm, [ready, free])
            done(t)
            if topk:
                ci, cut, cfree = self.ring["below"].take()
                t = p.op("act", lambda e: e.activation(cut[0:kc, :], ps[0:kc, :], ACT.Relu, scale=-STEEP), [t, cfree])
                return c, kc, i, ps, t, ci, cut
            return c, kc, i, ps, t, None, None

        def weights(c, kc, i, ps, t, ci, cut):
            if topk:
                def mm(e):
                    for b in range(0, HG * S, BANK):
                        r = e.matmul(ps[0:kc, b:b + BANK], m.minus_ident[0:kc, 0:kc], cut[0:kc, b:b + BANK],
                                     start=False, stop=True, skip_group_check=True)
                    return r
                t = p.op("pe", mm, [t])
                self.ring["below"].release(ci, t)
            pi, pr, pfree = self.ring["prob"].take()
            t = p.op("act", lambda e: e.activation(pr[0:kc, :], ps[0:kc, :], ACT.Exp, scale=SCALE), [t, pfree])
            self.ring["wide"].release(i, t)
            pend.append((c, kc, pi, pr, t))
        chunks, lot = list(range(-(-nk // P))), 2 if topk else 1
        for c in range(0, len(chunks), lot):
            made = [scores(cc) for cc in chunks[c:c + lot]]
            while pend:
                sums()
            for x in made:
                weights(*x)
            yield step * lot
        while len(pend) > 1:
            sums()
        last = sums()
        t0 = p.op("act", lambda e: e.activation(z["u"][:, :], ap[:, 0:S], ACT.Copy), [last, z["u_free"]])
        self.ring["att"].release(ai, t0)
        yield step
        i, ps, free = self.ring["small"].take()

        def tr(e):
            for t in range(QT):
                r = e.transpose(ps[:, t * P:(t + 1) * P], z["u"][:, t * P:(t + 1) * P], m.ident[:, :])
            return r
        t1 = p.op("pe", tr, [t0, free])
        z["u_free"] = t1
        pv = ps[:, 0:QT * P].rearrange("p (t j r) -> p t j r", t=QT, j=HG)
        t2 = p.op("dve", lambda e: e.reciprocal(z["rec"][:, :, :], pv[:, :, :, HD]), [t1])

        def mul(e):
            for t in range(QT):
                o = z["o"][:, t, g * HG * HD:(g + 1) * HG * HD].rearrange("p (j r) -> p j r", j=HG)
                r = e.tensor_tensor(o, pv[:, t, :, 0:HD], z["rec"][:, t, :].unsqueeze(2).to_broadcast([P, HG, HD]),
                                    ALU.mult)
            return r
        z["o_ready"] = p.op("dve", mul, [t2])
        self.ring["small"].release(i, z["o_ready"])

    def stage_attend(self, l, i, step):
        p, m, d, z = self.p, self.m, self.d, self.m.z["att%d" % l]
        z["u_free"] = None
        name = "att%d" % l
        xs, xd = (d.x[i, :, :].rearrange("(t p) d -> p t d", p=P), d.x0[i]) if l == 0 else (d.x1[i], d.x2[i])
        kring, qring = self.ring["k_" + name], self.ring["q_" + name]
        KB = 4

        def load_q(g):
            n, q, free = qring.take()
            t = p.dma(f"q_{name}_{n}", [
                (q[0:ROWS, :, :], d.q_stack[l][i, :, :, g * HG:(g + 1) * HG, :].rearrange("n j h s -> (n j) h s")),
                (q[ROWS:ROWX, :, :].rearrange("k h s -> k (h s)"), d.rows[l][i, :, g, :, :].rearrange("k a s -> k (a s)"))],
                [free])
            return n, q, t

        def load_k(g, b):
            n, k, free = kring.take()
            a, w = b * KB * P, min(KB * P, NK - b * KB * P)
            t = p.dma(f"k_{name}_{n}", [(k[0:ROWS, :, 0:w], d.k_stack[l][i, :, :, g * HG:(g + 1) * HG, a:a + w]
                                         .rearrange("n j h s -> (n j) h s"))], [free])
            return n, k, t
        blocks = [(g, b) for g in range(G) for b in range(-(-NC // KB))]
        qs = [load_q(0)]
        ks = [load_k(*blocks.pop(0))]
        v_ready = p.dma(name + "_v", [(m.v[l][:, :, :, :].rearrange("p c h j -> p c (h j)")[:, 0:NC - 1, :],
                                       d.v[l][i, :, 0:NC - 1, :]),
                                      (m.v[l][0:chunk(NK, NC - 1), NC - 1, :, :].rearrange("p h j -> p (h j)"),
                                       d.v[l][i, 0:chunk(NK, NC - 1), NC - 1, :])])
        x_ready = p.dma(name + "_x", [(z["x"][:, :, :], xs)])
        ks.append(load_k(*blocks.pop(0)))
        yield 2
        for g in range(G):
            if g + 1 < G:
                qs.append(load_q(g + 1))
            qn, q, q_ready = qs.pop(0)
            cur = {}

            def kq(c):
                if c % KB == 0:
                    cur["k"] = ks.pop(0)
                n, k, ready = cur["k"]

                def done(t):
                    if c % KB == KB - 1 or c == NC - 1:
                        kring.release(n, t)
                        if blocks:
                            ks.append(load_k(*blocks.pop(0)))
                    if c == NC - 1:
                        qring.release(qn, t)
                return k, q, c % KB * P, [ready, q_ready, v_ready], done
            yield from self.weigh(g, NK, kq, m.v[l], l == 1, step, g == G - 1, z)
            yield step
        yield 1
        t = self.turn(z["o"], z["oT"], z["o_ready"])
        yield 1
        n, ps, free = self.ring["small"].take()

        def mm(e):
            for q in range(QT):
                e.matmul(ps[:, q * D:(q + 1) * D], z["oT"][:, q * P:(q + 1) * P], m.w_oT[:, l, :], start=True, stop=False)
                r = e.matmul(ps[:, q * D:(q + 1) * D], m.ones[:, :], m.b_o[:, l, :], start=False, stop=True)
            return r
        t = p.op("pe", mm, [t, free])
        t = p.op("dve", lambda e: e.scalar_tensor_tensor(flat(z["x"]), ps[:, 0:QT * D], m.gates[:, l:l + 1], flat(z["x"]),
                                                         ALU.mult, ALU.add), [t, x_ready])
        self.ring["small"].release(n, t)
        p.dma(name + "_out", [(xd, z["x"][:, :, :])], [t])

    def route(self, z, w, bias, over_all):
        p, m = self.p, self.m
        i, ps, free = self.ring["small"].take()

        def mm(e):
            for t in range(QT):
                e.matmul(ps[:, t * E:(t + 1) * E], z["xnT"][:, t * P:(t + 1) * P], w[:, :], start=True, stop=False)
                r = e.matmul(ps[:, t * E:(t + 1) * E], m.ones[:, :], bias[:, :], start=False, stop=True)
            return r
        t = p.op("pe", mm, [z["xnT_ready"], free])
        t = p.op("dve", lambda e: e.tensor_copy(flat(z["s"]), ps[:, 0:QT * E]), [t])
        self.ring["small"].release(i, t)

        def best(e):
            for q in range(QT):
                r = e.max(z["best"][:, q, :], z["s"][:, q, :])
            return r
        t = p.op("dve", best, [t])

        def where(e):
            for q in range(QT):
                r = e.max_index(z["at"][:, q, :], z["best"][:, q, :], z["s"][:, q, :])
            return r
        t = p.op("dve", where, [t])
        t = p.op("dve", lambda e: e.tensor_copy(z["atf"][:, :, :], z["at"][:, :, :]), [t])
        t = p.op("dve", lambda e: e.tensor_scalar(z["neg"][:, :], z["best"][:, :, 0], -1.0, None, ALU.mult), [t])
        yield 1

        def ex(e):
            for q in range(QT):
                r = e.activation(z["e"][:, q, :], z["s"][:, q, :], ACT.Exp, bias=z["neg"][:, q:q + 1])
            return r
        t = p.op("act", ex, [t])
        yield 1

        def pick(k, dst):
            def f(e):
                for q in range(QT):
                    r = e.scalar_tensor_tensor(dst[:, q, :], m.iota8[:, :], z["atf"][:, q, k:k + 1], z["e"][:, q, :],
                                               ALU.is_equal, ALU.mult)
                return r
            return f
        p.op("dve", pick(0, z["w"]), [t])
        t = p.op("dve", pick(1, z["w2"]))
        t = p.op("dve", lambda e: e.tensor_tensor(z["w"][:, :, :], z["w"][:, :, :], z["w2"][:, :, :], ALU.add), [t])
        whole = z["e"] if over_all else z["w"]
        t = p.op("dve", lambda e: e.tensor_reduce(z["sum"][:, :], whole[:, :, :], AX.X, ALU.add), [t])
        t = p.op("dve", lambda e: e.reciprocal(z["sum"][:, :], z["sum"][:, :]), [t])

        def fin(e):
            for q in range(QT):
                r = e.tensor_scalar(z["w"][:, q, :], z["w"][:, q, :], z["sum"][:, q:q + 1], None, ALU.mult)
            return r
        z["w_ready"] = p.op("dve", fin, [t])

    def add_expert(self, z, n, y, first, after):
        def f(e):
            for q in range(QT):
                w = z["w"][:, q, n:n + 1]
                if first:
                    r = e.tensor_scalar(z["acc"][:, q, :], y(q), w, None, ALU.mult)
                else:
                    r = e.scalar_tensor_tensor(z["acc"][:, q, :], y(q), w, z["acc"][:, q, :], ALU.mult, ALU.add)
            return r
        return self.p.op("dve", f, after)

    def gated(self, z, gate, ready):
        return self.p.op("dve", lambda e: e.scalar_tensor_tensor(
            flat(z["x"]), flat(z["acc"]), self.m.gates[:, gate:gate + 1], flat(z["x"]), ALU.mult, ALU.add), [ready])

    def stage_v(self, i, step):
        p, m, d, z = self.p, self.m, self.d, self.m.z["v"]
        x = p.dma("v_x", [(z["x"][:, :, :], d.x0[i])])
        yield 2
        yield from self.norm(z, x)
        yield 1
        yield from self.route(z, m.w_r, m.b_r, False)
        yield 1
        acc = None
        for e0 in range(0, E, 2):
            hs = []
            while not self.ring["hid"].ready(2):
                yield 0.25
            for x_ in (e0, e0 + 1):
                n, ps, free = self.ring["wide"].take()

                def mm(e):
                    for k in range(PT):
                        r = e.matmul(ps[:, k * S:(k + 1) * S], m.w_1[:, x_, k * P:(k + 1) * P], z["xnT"][:, :],
                                     start=True, stop=True)
                    return r
                t0 = p.op("pe", mm, [z["xnT_ready"], free])
                hs.append((x_, n, ps, t0))
            hid = []
            for x_, n, ps, t0 in hs:
                hn, hb, hfree = self.ring["hid"].take()

                def gl(e):
                    for k in range(PT):
                        r = e.activation(hb[:, k, :], ps[:, k * S:(k + 1) * S], ACT.Gelu_apprx_tanh,
                                         bias=m.b_1[:, x_, k:k + 1])
                    return r
                t1 = p.op("act", gl, [t0, hfree])
                self.ring["wide"].release(n, t1)
                hid.append((x_, hn, hb, t1))
            yield step / 2
            for x_, hn, hb, t1 in hid:
                n, ps, free = self.ring["small"].take()

                def mm2(e):
                    for q in range(QT):
                        e.matmul(ps[:, q * D:(q + 1) * D], m.ones[:, :], m.b_2[:, x_ * D:(x_ + 1) * D], start=True, stop=False)
                        for k in range(PT):
                            r = e.matmul(ps[:, q * D:(q + 1) * D], hb[:, k, q * P:(q + 1) * P], m.w_2[:, x_, k, :],
                                         start=False, stop=(k == PT - 1))
                    return r
                t2 = p.op("pe", mm2, [t1, free])
                self.ring["hid"].release(hn, t2)
                acc = self.add_expert(z, x_, lambda q: ps[:, q * D:(q + 1) * D], x_ == 0, [t2, z["w_ready"], acc])
                self.ring["small"].release(n, acc)
                yield step
        t = self.gated(z, 2, acc)
        p.dma("v_out", [(d.x1[i], z["x"][:, :, :])], [t])
        yield 1
        yield from self.norm(z, t)
        yield 1
        self.to_stack(m.w_qT[:, 1, :], z["xnT"][:, :], m.b_q[:, 1:2], S, d.q_stack[1][i], QPART, slice(0, S), z["xnT_ready"])

    def stage_z(self, i, step):
        p, m, d, z = self.p, self.m, self.d, self.m.z["z"]
        z["u_free"] = z["sent"] = z["src_free"] = None
        x = p.dma("z_x", [(z["x"][:, :, :], d.x2[i])])
        yield 2
        yield from self.norm(z, x)
        yield 1
        sent = [self.to_stack(m.w_qkv[:, n, :], z["xnT"][:, :], m.b_qk[:, n:n + 1], S, d.self_stack[n][i],
                              (QPART, KPART)[n], slice(0, S), z["xnT_ready"]) for n in range(2)]
        n, ps, free = self.ring["small"].take()

        def mm(e):
            for q in range(QT):
                e.matmul(ps[:, q * D:(q + 1) * D], z["xnT"][:, q * P:(q + 1) * P], m.w_qkv[:, 2, :], start=True, stop=False)
                r = e.matmul(ps[:, q * D:(q + 1) * D], m.ones[:, :], m.b_v2[:, :], start=False, stop=True)
            return r
        t = p.op("pe", mm, [z["xnT_ready"], free])
        v_ready = p.op("act", lambda e: e.activation(m.v[2][:, :, :, 0:HD].rearrange("p t h j -> p (t h) j"),
                                                     ps[:, 0:QT * D].rearrange("p (c j) -> p c j", j=HD), ACT.Copy), [t])
        self.ring["small"].release(n, v_ready)
        yield 1
        yield from self.route(z, m.w_g, m.b_g, True)
        yield 1
        acc = None
        for q in range(QT):
            while not self.ring["hid"].ready(1):
                yield 0.25
            n, ps, free = self.ring["wide"].take()

            def mm3(e):
                for b in range(0, E * D, BANK):
                    e.matmul(ps[:, b:b + BANK], z["xnT"][:, q * P:(q + 1) * P], m.w_e[:, b:b + BANK], start=True, stop=False)
                    r = e.matmul(ps[:, b:b + BANK], m.ones_e[:, :], m.b_e[:, b:b + BANK], start=False, stop=True)
                return r
            t = p.op("pe", mm3, [z["xnT_ready"], free])
            yi, y, yfree = self.ring["hid"].take()
            t = p.op("act", lambda e: e.activation(y[:, :, :].rearrange("p a b -> p (a b)"), ps[:, :], ACT.Copy), [t, yfree])
            self.ring["wide"].release(n, t)
            yf = y[:, :, :].rearrange("p a b -> p (a b)")
            for n in range(E):
                w = z["w"][:, q, n:n + 1]
                yn = yf[:, n * D:(n + 1) * D]
                if n == 0:
                    t = p.op("dve", lambda e: e.tensor_scalar(z["acc"][:, q, :], yn, w, None, ALU.mult), [t, z["w_ready"]])
                else:
                    t = p.op("dve", lambda e: e.scalar_tensor_tensor(z["acc"][:, q, :], yn, w, z["acc"][:, q, :], ALU.mult,
                                                                     ALU.add), [t])
            self.ring["hid"].release(yi, t)
            acc = t
            yield step
        for g in range(G):
            hs = slice(g * HG, (g + 1) * HG)
            n, (kt, qt_), free = self.ring["kq_self"].take()
            t0 = p.dma(f"kq_self{n}", [(kt[0:ROWS, :, :], d.self_stack[1][i, :, :, hs, :].rearrange("n j h s -> (n j) h s")),
                                       (qt_[0:ROWS, :, :], d.self_stack[0][i, :, :, hs, :].rearrange("n j h s -> (n j) h s"))],
                       [sent, free])
            yield step
            for h in range(HG):
                si, ps, sfree = self.ring["score"].take()

                def mm4(e):
                    for q in range(QT):
                        r = e.matmul(ps[:, q * S:(q + 1) * S], qt_[0:ROWS, h, q * P:(q + 1) * P], kt[0:ROWS, h, :],
                                     start=True, stop=True)
                    return r
                t1 = p.op("pe", mm4, [t0, sfree])
                t2 = p.op("dve", lambda e: e.tensor_reduce(z["mx"][:, h * QT:(h + 1) * QT],
                                                           ps[:, :].rearrange("p (q s) -> p q s", q=QT), AX.X, ALU.max),
                          [t1, z["src_free"]])
                self.ring["score"].release(si, t2)
                yield step / 2
            t3 = self.shift_rows(z, z["mx"], i, g, d.rows[2], t2, "z_rows")
            t4 = p.dma(f"z_rows_in{n}", [(qt_[ROWS:ROWX, :, :].rearrange("k h s -> k (h s)"),
                                          d.rows[2][i, :, g, :, :].rearrange("k a s -> k (a s)"))], [t3])
            yield Z_WAIT

            def kq(c):
                def done(t):
                    if c == QT - 1:
                        self.ring["kq_self"].release(n, t)
                return kt, qt_, c * P, [t4, v_ready], done
            yield from self.weigh(g, S, kq, m.v[2], False, 0.4, g == G - 1, z)
            yield 1
        t = p.op("dve", lambda e: e.tensor_tensor(flat(z["acc"]), flat(z["acc"]), flat(z["o"]), ALU.add), [acc, z["o_ready"]])
        t = self.gated(z, 3, t)
        p.dma("z_out", [(d.out[i, :, :].rearrange("(t p) d -> p t d", p=P), z["x"][:, :, :])], [t])


def flat(x):
    return x[:, :, :].rearrange("p t d -> p (t d)")


class Buffers:
    pass


class Dram:
    pass


def build(nc, a, out):
    ctx = ExitStack()
    with ctx, nc.allow_non_contiguous_dma(reason="small strided parts of weights and biases"):
        def sb(name, shape, dt=F32):
            return ctx.enter_context(nc.sbuf_tensor(name, shape, dt))

        def psum(name, n):
            return ctx.enter_context(nc.psum_tensor(name, [P, n], F32))
        m, d = Buffers(), Dram()
        m.ident, m.ones_rows = sb("ident", [P, P]), sb("ones_rows", [33, P])
        m.ones, m.ones_e = m.ones_rows[0:1, :], m.ones_rows[32:33, :]
        m.minus_ident = sb("minus_ident", [P, P], BF16)
        m.iota8, m.half = sb("iota8", [P, E]), sb("half", [P, QT])
        m.gates = sb("gates", [P, 4])
        m.w_kT, m.w_qT, m.w_vT, m.w_oT = (sb(n, [P, 2, D]) for n in ("w_kT", "w_qT", "w_vT", "w_oT"))
        m.b_q, m.b_k, m.b_v, m.b_o = sb("b_q", [P, 2]), sb("b_k", [P, 2]), sb("b_v", [P, 2]), sb("b_o", [1, 2, D])
        m.w_1, m.b_1 = sb("w_1", [P, E, FF]), sb("b_1", [P, E, PT])
        m.w_2, m.b_rows = sb("w_2", [P, E, PT, D]), sb("b_rows", [33, E * D])
        m.b_2, m.b_e = m.b_rows[0:1, :], m.b_rows[32:33, :]
        m.w_r, m.b_r, m.w_g, m.b_g = sb("w_r", [P, E]), sb("b_r", [1, E]), sb("w_g", [P, E]), sb("b_g", [1, E])
        m.w_qkv, m.b_qk, m.b_v2 = sb("w_qkv", [P, 3, D]), sb("b_qk", [P, 2]), sb("b_v2", [1, D])
        m.w_e = sb("w_e", [P, E * D])

        def dram(name, shape, dt=F32):
            return nc.dram_tensor(name, shape, dt).ap()
        d.x, d.ctx, d.out = a["x"], a["ctx_1024"], out
        d.k_stack = [dram(f"k_stack{l}", (B, NT, HD, H, NK), BF16) for l in range(2)]
        d.q_stack = [dram(f"q_stack{l}", (B, NT, HD, H, S), BF16) for l in range(2)]
        d.self_stack = [dram(f"self_stack{n}", (B, NT, HD, H, S), BF16) for n in range(2)]
        d.rows = [dram(f"rows{l}", (B, 3, G, HG * QT, P), BF16) for l in range(3)]
        d.v = [dram(f"v_dram{l}", (B, P, NC, H * (HD + 1))) for l in range(2)]
        d.x0, d.x1, d.x2 = (dram(n, (B, P, QT, D)) for n in ("x0", "x1", "x2"))

        m.ctxT = sb("ctxT", [P, NK])
        m.v = [sb("v0", [P, NC, H, HD + 1]), sb("v1", [P, NC, H, HD + 1]), sb("v2", [P, QT, H, HD + 1])]
        m.cut, m.top = sb("cut", [P, NK]), sb("top", [P, TOPK // 8, 8])
        m.rings = {
            "wide": [psum(f"wide{n}", 2 * BANK) for n in range(2)],
            "score": [psum(f"score{n}", BANK) for n in range(2)],
            "att": [psum("att", BANK)],
            "small": [psum("small", BANK)],
            "split": [(sb(f"split_f{n}", [P, BANK]), sb(f"split_b{n}", [P, 3, BANK], BF16)) for n in range(2)],
            "v_out": [sb(f"v_out{n}", [P, 4 * H, HD + 1]) for n in range(2)],
            "s": [sb(f"s{n}", [P, NK]) for n in range(2)],
            "below": [sb(f"below{n}", [P, HG * S], BF16) for n in range(2)],
            "prob": [sb(f"prob{n}", [P, HG * S]) for n in range(3)],
            "hid": [sb(f"hid{n}", [P, PT, S]) for n in range(2)],
            "kq_self": [(sb(f"k_self{n}", [64, HG, S], BF16), sb(f"q_self{n}", [64, HG, S], BF16)) for n in range(1)],
        }
        for l in range(2):
            m.rings[f"k_scan{l}"] = [sb(f"k_scan{l}_{n}", [ROWS, NK], BF16) for n in range(2)]
            m.rings[f"q_scan{l}"] = [sb(f"q_scan{l}_{n}", [ROWS, HG, S], BF16) for n in range(2)]
            m.rings[f"k_att{l}"] = [sb(f"k_att{l}_{n}", [64, HG, 4 * P], BF16) for n in range(2)]
            m.rings[f"q_att{l}"] = [sb(f"q_att{l}_{n}", [64, HG, S], BF16) for n in range(2)]
        m.z = {}

        def state(name, **shapes):
            m.z[name] = {k: sb(f"{name}_{k}", shape, dt) for k, (shape, dt) in shapes.items()}
        NORM = dict(x=([P, QT, D], F32), xn=([P, QT, D], F32), xnT=([P, S], F32), stats=([P, QT, 6], F32),
                    mv=([P, QT, 2], F32), rstd=([P, QT], F32))
        SHIFT = dict(mx=([P, HG * QT], F32), minus=([8, P], F32), res=([8, P], F32), shift=([8, 3, P], BF16))
        SUM = dict(u=([P, S], F32), rec=([P, QT, HG], F32), o=([P, QT, D], F32))
        ROUTE = dict(s=([P, QT, E], F32), best=([P, QT, 8], F32), at=([P, QT, 8], U32), atf=([P, QT, 8], F32),
                     e=([P, QT, E], F32), w=([P, QT, E], F32), w2=([P, QT, E], F32), sum=([P, QT], F32),
                     acc=([P, QT, D], F32))
        state("w", **NORM)
        state("scan0", part=([P, HG * QT, 4], F32), **SHIFT)
        state("scan1", kth=([P, HG * QT], F32), th=([P, HG * QT], F32), **SHIFT)
        for l in range(2):
            state(f"att{l}", x=([P, QT, D], F32), oT=([P, S], F32), **SUM)
        state("v", neg=([P, QT], F32), **NORM, **ROUTE)
        state("z", neg=([P, QT], F32), **NORM, **SHIFT, **SUM, **ROUTE)
        sems = {k: ctx.enter_context(nc.semaphore(f"{k}_done")) for k in ("pe", "act", "dve", "pool")}
        dma_sems = [ctx.enter_context(nc.semaphore(f"dma_done{n}")) for n in range(48)]
        nums = [s.num for s in list(sems.values()) + dma_sems]
        assert max(nums) - min(nums) + 1 == len(nums)

        def end_pass(p):
            p.run()
            nc.all_engine_barrier(sems_to_clear=range(min(nums), max(nums) + 1))

        p = Pass(nc, sems, dma_sems)
        row = lambda name: a[name].rearrange("(o n) -> o n", o=1)
        col = lambda name: a[name].rearrange("(p o) -> p o", o=1)
        loads = []
        for l, pre in enumerate(("L0_xattn_", "L1_xattn_")):
            loads += [(m.w_kT[:, l, :], a[pre + "Wk"]), (m.w_qT[:, l, :], a[pre + "Wq"]),
                      (m.w_vT[:, l, :], a[pre + "Wv"]), (m.w_oT[:, l, :], a[pre + "Wo"]),
                      (m.b_q[:, l:l + 1], col(pre + "bq")), (m.b_k[:, l:l + 1], col(pre + "bk")),
                      (m.b_v[:, l:l + 1], col(pre + "bv")), (m.b_o[:, l, :], row(pre + "bo"))]
        loads += [(m.w_1[:, :, :], a["L0_ffn_W1"].rearrange("e d f -> d e f")),
                  (m.b_2[:, :], a["L0_ffn_b2"].rearrange("(o e) d -> o (e d)", o=1)),
                  (m.w_r[:, :], a["L0_ffn_Wr"]), (m.b_r[:, :], row("L0_ffn_br")),
                  (m.w_qkv[:, :, :], a["L1_ffn_W_qkv"].rearrange("d (n f) -> d n f", n=3)),
                  (m.b_v2[:, :], row("L1_ffn_b_qkv")[:, 2 * D:3 * D]),
                  (m.w_g[:, :], a["L1_ffn_W_gate"]), (m.b_g[:, :], row("L1_ffn_b_gate")),
                  (m.w_e[:, :].rearrange("p (e f) -> p e f", e=E), a["L1_ffn_W_experts"].rearrange("e d f -> d e f")),
                  (m.b_e[:, :], a["L1_ffn_b_experts"].rearrange("(o e) f -> o (e f)", o=1)),
                  (m.gates[:, 0:2], row("g_xattn").to_broadcast([P, 2])),
                  (m.gates[:, 2:4], row("g_ffn").to_broadcast([P, 2]))]
        loads += [(m.b_qk[:, n:n + 1], a["L1_ffn_b_qkv"][n * D:(n + 1) * D].rearrange("(p o) -> p o", o=1))
                  for n in range(2)]
        for e_ in range(E):
            loads += [(m.b_1[:, e_, :], a["L0_ffn_b1"][e_, :].rearrange("(t p) -> p t", p=P)),
                      (m.w_2[:, e_, :, :], a["L0_ffn_W2"][e_, :, :].rearrange("(t p) d -> p t d", p=P))]
        loaded = p.dma("weights", loads)
        t = p.op("pool", lambda e: e.memset(m.ident[:, :], 0.0))
        p.op("pool", lambda e: e.affine_select(out=m.ident[:, :], in_=m.ident[:, :], compare_op=ALU.not_equal,
                                               fill=1.0, base=0, pattern=[[-1, P]], channel_multiplier=1), [t])
        t = p.op("pool", lambda e: e.memset(m.minus_ident[:, :], 0.0))
        p.op("pool", lambda e: e.affine_select(out=m.minus_ident[:, :], in_=m.minus_ident[:, :],
                                               compare_op=ALU.not_equal, fill=-1.0, base=0, pattern=[[-1, P]],
                                               channel_multiplier=1), [t])
        for j in range(E):
            p.op("pool", lambda e: e.memset(m.iota8[:, j:j + 1], float(j)))
        p.op("pool", lambda e: e.memset(m.half[:, :], -0.5))
        p.op("pool", lambda e: e.memset(m.ones_rows[:, :], 1.0))
        for buf in (*m.rings["k_att0"], *m.rings["k_att1"], m.rings["kq_self"][0][0]):
            p.op("pool", lambda e: e.memset(buf[:, :, :], 1.0))
        for buf in (*m.rings["v_out"],):
            p.op("pool", lambda e: e.memset(buf[:, :, :], 1.0))
        p.op("pool", lambda e: e.memset(m.v[2][:, :, :, :], 1.0))
        att, u = m.rings["att"][0], m.z["z"]["u"]
        t = p.op("dve", lambda e: e.memset(u[:, :], 0.0))
        p.op("pe", lambda e: e.matmul(att[:, 0:S], u[:, 0:P], u[:, :], start=True, stop=True), [t])
        p.op("act", lambda e: e.activation(m.gates[:, :], m.gates[:, :], ACT.Tanh), [loaded])
        small = m.rings["small"][0]
        for l in range(2):
            t = p.op("pe", lambda e: e.matmul(small[0:1, l * D:(l + 1) * D], m.b_v[:, l:l + 1], m.w_oT[:, l, :],
                                              start=True, stop=True), [loaded, t if l else None])
            t = p.op("dve", lambda e: e.tensor_tensor(m.b_o[:, l, :], small[0:1, l * D:(l + 1) * D], m.b_o[:, l, :],
                                                      ALU.add), [t])
        end_pass(p)

        AFTER = dict(w=0, scan0=1, att0=2, v=3, scan1=4, att1=5, z=6)
        DEPTH = max(AFTER.values())

        def one_pass(n, active):
            p = Pass(nc, sems, dma_sems)
            s = Stages(p, m, d)
            make = dict(w=lambda i: (0, s.stage_w(i)), scan0=lambda i: (0.3, s.stage_scan(0, i, SCAN0)),
                        att0=lambda i: (ATT0_AT, s.stage_attend(0, i, ATT0)), v=lambda i: (V_AT, s.stage_v(i, V_STEP)),
                        scan1=lambda i: (0.1, s.stage_scan(1, i, SCAN1)),
                        att1=lambda i: (0.2, s.stage_attend(1, i, ATT1)),
                        z=lambda i: (Z_AT, s.stage_z(i, Z_STEP)))
            for name, k in AFTER.items():
                if name in active:
                    p.stage(*make[name](n - k))
            end_pass(p)
        for n in range(DEPTH):
            one_pass(n, [k for k, v in AFTER.items() if n >= v])
        with nc.Fori(DEPTH, B) as n:
            one_pass(n, list(AFTER))
        for n in range(B, B + DEPTH):
            one_pass(n, [k for k, v in AFTER.items() if n - v < B])


_OUTS = [((B, S, D), "float32")]


def kernel(**inputs):
    import numpy as _np
    import concourse.bacc as _bacc
    from concourse import mybir as _mybir
    from concourse.bass_utils import run_bass_kernel_spmd as _run

    nc = _bacc.Bacc("TRN2", target_bir_lowering=False, num_devices=1)
    arrays, args = {}, {}
    for name in inputs:
        v = _np.asarray(inputs[name])
        if name == "ctx_1024":
            v = v.transpose(0, 2, 1)
        elif name.split("_")[-1] in ("Wq", "Wk", "Wv", "Wo"):
            v = v.T
        v = _np.ascontiguousarray(v)
        arrays[f"in_{name}_dram"] = v
        args[name] = nc.dram_tensor(f"in_{name}_dram", v.shape, _mybir.dt.from_np(v.dtype), kind="ExternalInput").ap()
    outs = [nc.dram_tensor(f"out_{i}_dram", shape, _mybir.dt.from_np(_np.dtype(dtype)), kind="ExternalOutput").ap()
            for i, (shape, dtype) in enumerate(_OUTS)]
    build(nc, args, outs[0])
    r = _run(nc, [arrays], core_ids=[0])
    return r.results[0]["out_0_dram"]
```

```python
import numpy as np
import concourse.bass as bass
import concourse.mybir as mybir
from concourse.alu_op_type import AluOpType as ALU
from contextlib import ExitStack

F32 = mybir.dt.float32
BF16 = mybir.dt.bfloat16
U32 = mybir.dt.uint32
I32 = mybir.dt.int32
ACT = mybir.ActivationFunctionType
AX = mybir.AxisListType

B, S, D = 16, 256, 128
NK = 1601
H, HD = 16, 8
P = 128
QT = S // P
G, HG = 4, 4
E, FF = 8, 512
PT = FF // P
TOPK = 32
NC = -(-NK // P)
KC = 24
KCUT = [round(c * NK / KC) for c in range(KC + 1)]
BANK = 512
SCALE = float(1.0 / np.sqrt(HD))
EPS = 1e-5
NEG = -3.0e38
STEEP = 2.0 ** 66
GUARD = 60.0 / SCALE
ROUND = 2.0 ** -21

KPART = (0, 0, 0, 1, 1, 2)
QPART = (0, 1, 2, 0, 1, 0)
NT = len(KPART)
ROWS = NT * HD
ROWX = ROWS + 3


W_STEP = 3
SCAN0, ATT0, ATT0_AT, V_AT, V_STEP, SCAN1, ATT1, Z_AT, Z_STEP = 2.3, 1.1, 0.4, 1, 5, 2.2, 1.25, 1, 1


SLOT, LATENCY, GAP, DMA_EACH, DMA_WAY = 3.5, 0.2, 0.1, 0.55, 2.5
AHEAD = 3


def chunk(n, c):
    return min(P, n - c * P)


class Pass:

    def __init__(self, nc, sems, dma_sems):
        self.eng = {"pe": nc.tensor, "act": nc.scalar, "dve": nc.vector, "pool": nc.gpsimd, "sp": nc.sync}
        self.sem = sems
        self.count = {k: 0 for k in sems}
        self.dma_sem, self.streams = list(dma_sems), {}
        self.seen, self.stages = {}, []
        self.now, self.through, self.reached, self.last = 0.0, {}, {}, 0.0

    def wait(self, name, tokens):
        for t in tokens:
            if isinstance(t, list):
                self.wait(name, t)
            elif t is not None and self.seen.get((name, t[0]), 0) < t[1]:
                self.seen[(name, t[0])] = t[1]
                self.eng[name].wait_ge(t[2], t[1])

    def plan(self, name, us, after):
        at = max(self.now, self.through.get(name, 0.0), self.when(after))
        self.through[name] = self.last = at + us
        return at + us

    def when(self, tokens):
        if isinstance(tokens, tuple) and tokens and isinstance(tokens[0], str):
            return self.reached.get(tokens[:2], 0.0) + LATENCY
        return max([self.when(t) for t in tokens if t is not None], default=0.0) if tokens else 0.0

    def op(self, name, fn, after=(), us=0.3, alone=False):
        if name in ("dve", "pool") and self.count[name] and not alone:
            self.wait(name, [(name, self.count[name], self.sem[name])])
        self.wait(name, after)
        fn(self.eng[name]).then_inc(self.sem[name], 1)
        self.count[name] += 1
        self.reached[(name, self.count[name])] = self.plan(name, us + (GAP if name in ("dve", "pool") and not alone else 0), after)
        return (name, self.count[name], self.sem[name])

    def dma(self, stream, copies, after=()):
        if stream not in self.streams:
            self.streams[stream] = [self.dma_sem[len(self.streams)], 0]
        s = self.streams[stream]
        self.wait("sp", after)
        for out, in_ in copies:
            self.eng["sp"].dma_start(out, in_).then_inc(s[0], 16)
            s[1] += 16
        self.reached[(stream, s[1])] = self.plan("sp", DMA_EACH * len(copies), after) + DMA_WAY
        return (stream, s[1], s[0])

    def stage(self, at, gen):
        self.stages.append((at * SLOT, len(self.stages), gen, at))

    def run(self):
        while self.stages:
            self.stages.sort(key=lambda s: s[:2])
            at, n, gen, slots = self.stages.pop(0)
            self.now, self.last = max(self.now, at), 0.0
            step = next(gen, None)
            if step is not None:
                step, tokens = step if isinstance(step, tuple) else (step, None)
                slots += step
                at = max(slots * SLOT, self.when([tokens]), self.last - AHEAD)
                self.stages.append((at, n, gen, slots))
        for stream, (sem, total) in self.streams.items():
            self.wait("sp", [(stream, total, sem)])


class Ring:

    def __init__(self, bufs):
        self.bufs, self.n = bufs, 0
        self.free, self.held = [None] * len(bufs), [False] * len(bufs)

    def take(self):
        i = self.n % len(self.bufs)
        self.n += 1
        assert not self.held[i]
        self.held[i] = True
        return i, self.bufs[i], self.free[i]

    def ready(self, k):
        return not any(self.held[(self.n + j) % len(self.bufs)] for j in range(k))

    def next_free(self):
        return self.free[self.n % len(self.bufs)]

    def release(self, i, *tokens):
        assert self.held[i]
        self.free[i], self.held[i] = list(tokens), False


class Stages:

    def __init__(self, p, m, d):
        self.p, self.m, self.d = p, m, d
        self.ring = {k: Ring(v) for k, v in m.rings.items()}

    def turn(self, src, dst, ready):
        p, m = self.p, self.m
        i, ps, free = self.ring["small"].take()

        def tr(e):
            for t in range(QT):
                r = e.transpose(ps[:, t * P:(t + 1) * P], src[:, t, :], m.ident[:, :])
            return r
        t0 = p.op("pe", tr, [ready, free])
        t1 = p.op("act", lambda e: e.activation(dst[:, :], ps[:, 0:S], ACT.Copy), [t0])
        self.ring["small"].release(i, t1)
        return t1

    def norm(self, z, ready):
        p, m = self.p, self.m

        def stats(e):
            for t in range(QT):
                r = e.bn_stats(z["stats"][:, t, :], z["x"][:, t, :])
            return r
        t0 = p.op("dve", stats, [ready])

        def aggr(e):
            for t in range(QT):
                r = e.bn_aggr(z["mv"][:, t, :], z["stats"][:, t, :])
            return r
        t0 = p.op("dve", aggr, [t0])
        t0 = p.op("dve", lambda e: e.tensor_scalar_add(z["rstd"][:, :], z["mv"][:, :, 1], EPS), [t0])
        t0 = p.op("pool", lambda e: e.tensor_tensor(z["rstd"][:, :], z["rstd"][:, :], m.half[:, :], ALU.pow), [t0], 0.6)
        yield 0.2, t0

        def scale(e):
            for t in range(QT):
                r = e.tensor_scalar(z["xn"][:, t, :], z["x"][:, t, :], z["mv"][:, t, 0:1], z["rstd"][:, t:t + 1],
                                    ALU.subtract, ALU.mult)
            return r
        t0 = p.op("dve", scale, [t0])
        yield 0.2, t0
        z["xnT_ready"] = self.turn(z["xn"], z["xnT"], t0)

    def split(self, src, part, n, ready, free):
        p = self.p
        t = p.op("pool", lambda e: e.tensor_copy(part[:, 0, 0:n], src[:, 0:n]), [ready, free], n / 600)
        t = p.op("pool", lambda e: e.tensor_tensor(src[:, 0:n], src[:, 0:n], part[:, 0, 0:n], ALU.subtract), [t], n / 600)
        t = p.op("pool", lambda e: e.tensor_copy(part[:, 1, 0:n], src[:, 0:n]), [t], n / 600)
        return p.op("pool", lambda e: e.tensor_tensor(part[:, 2, 0:n], src[:, 0:n], part[:, 1, 0:n], ALU.subtract), [t], n / 600)

    def to_stack(self, w, rhs, bias, n, stack, parts, cols, ready):
        p = self.p
        i, ps, free = self.ring["wide"].take()
        t0 = p.op("pe", lambda e: e.matmul(ps[:, 0:n], w, rhs, start=True, stop=True), [ready, free], n / 600)
        fi, (f, part), ffree = self.ring["split"].take()
        t1 = p.op("act", lambda e: e.activation(f[:, 0:n], ps[:, 0:n], ACT.Identity, bias=bias), [t0, ffree], 0.2 + n / 1000)
        self.ring["wide"].release(i, t1)
        t2 = self.split(f, part, n, t1, ffree)
        t3 = p.dma(f"split{fi}", [(stack[k, :, :, cols].rearrange("j h s -> h j s"), part[:, parts[k], 0:n])
                                  for k in range(NT)], [t2])
        self.ring["split"].release(fi, t3)
        return t3

    def shift_rows(self, z, src, i, g, rows, ready, name):
        p, m = self.p, self.m
        n, ps, free = self.ring["small"].take()
        t = p.op("pe", lambda e: e.transpose(ps[0:8, 0:P], src[:, :], m.ident[:, :]), [ready, free])
        z["src_free"] = t
        t = p.op("act", lambda e: e.activation(z["minus"][:, :], ps[0:8, 0:P], ACT.Copy, scale=-1.0), [t])
        self.ring["small"].release(n, t)
        t = p.op("pool", lambda e: e.tensor_copy(z["shift"][:, 0, :], z["minus"][:, :]), [t, z["sent"]])
        t = p.op("pool", lambda e: e.tensor_tensor(z["res"][:, :], z["minus"][:, :], z["shift"][:, 0, :], ALU.subtract), [t])
        t = p.op("pool", lambda e: e.tensor_copy(z["shift"][:, 1, :], z["res"][:, :]), [t])
        t = p.op("pool", lambda e: e.tensor_tensor(z["shift"][:, 2, :], z["res"][:, :], z["shift"][:, 1, :], ALU.subtract), [t])
        z["sent"] = p.dma(name, [(rows[i, k, g, :, :], z["shift"][:, k, :]) for k in range(3)], [t])
        return z["sent"]

    def stage_w(self, i):
        p, m, d, z = self.p, self.m, self.d, self.m.z["w"]
        x = p.dma("w_x", [(z["x"][:, :, :], d.x[i, :, :].rearrange("(t p) d -> p t d", p=P))])
        yield 0.2, x
        c = p.dma("w_ctx", [(m.ctxT[:, :], d.ctx[i, :, :])])
        yield from self.norm(z, x)
        yield 0.2, z["xnT_ready"]
        self.to_stack(m.w_qT[:, 0, :], z["xnT"][:, :], m.b_q[:, 0:1], S, d.q_stack[0][i], QPART, slice(0, S), z["xnT_ready"])
        yield 1
        for l in range(2):
            for k in range(-(-NK // BANK)):
                a, w = k * BANK, min(BANK, NK - k * BANK)
                self.to_stack(m.w_kT[:, l, :], m.ctxT[:, a:a + w], m.b_k[:, l:l + 1], w, d.k_stack[l][i], KPART,
                              slice(a, a + w), c)
                yield W_STEP
                cs = range(4 * k, min(4 * k + 4, NC))
                n, ps, free = self.ring["wide"].take()

                def mm(e):
                    for q, cc in enumerate(cs):
                        kc = chunk(NK, cc)
                        r = e.matmul(ps[0:kc, q * D:(q + 1) * D], m.ctxT[:, cc * P:cc * P + kc], m.w_vT[:, l, :],
                                     start=True, stop=True)
                    return r
                t0 = p.op("pe", mm, [c, free])
                vi, vo, vfree = self.ring["v_out"].take()
                kc = chunk(NK, cs[-1])
                t1 = p.op("act", lambda e: e.activation(
                    vo[0:kc, 0:len(cs) * H, 0:HD], ps[0:kc, 0:len(cs) * D].rearrange("p (c j) -> p c j", j=HD),
                    ACT.Copy), [t0, vfree])
                self.ring["wide"].release(n, t1)
                t2 = p.dma(f"v_out{vi}", [(d.v[l][i, 0:kc, cs[0]:cs[-1] + 1, :],
                                           vo[0:kc, 0:len(cs) * H, :].rearrange("p (c h) j -> p c (h j)", h=H))], [t1])
                self.ring["v_out"].release(vi, t2)
                yield W_STEP

    def stage_scan(self, l, i, step):
        p, m, d, z = self.p, self.m, self.d, self.m.z["scan%d" % l]
        z["sent"] = z["src_free"] = read = None
        name = "scan%d" % l
        qring, kring = self.ring["q_" + name], self.ring["k_" + name]

        def load_q(g):
            n, q, free = qring.take()
            t = p.dma(f"q_{name}_{n}", [(q[0:ROWS, :, :], d.q_stack[l][i, :, :, g * HG:(g + 1) * HG, :]
                                         .rearrange("n j h s -> (n j) h s"))], [free])
            return n, q, t

        def load_k(h):
            n, k, free = kring.take()
            t = p.dma(f"k_{name}_{n}", [(k[0:ROWS, :], d.k_stack[l][i, :, :, h, :].rearrange("n j s -> (n j) s"))],
                      [free])
            return n, k, t
        z["read"] = None
        late = []

        def rank(span):
            new = late[-1] if late and late[-1]["flag"] is None else None
            old = late[0] if late and late[0]["flag"] is not None else None
            if new:
                yield from self.candidates(z, new["s"], new["ready"], span / 4)
            if old:
                late.pop(0)
                done = self.check(z, old)
                self.ring["s"].release(old["buf"], done)
                if old["n"] == HG * QT - 1:
                    last = self.threshold(z)
                    yield span / 8, last
                    self.shift_rows(z, z["th"], i, old["g"], d.rows[1], last, name + "_rows")
                yield span / 4
            if new:
                yield from self.kth(z, new, span / 4)
                z["read"] = new["flag"]
        qs, ks = [load_q(0)], [load_k(0)]
        yield 0.5
        ks.append(load_k(1))
        yield 0.1, ks[0][2]
        for g in range(G):
            if g + 1 < G:
                qs.append(load_q(g + 1))
            qn, q, q_ready = qs.pop(0)
            for hh in range(HG):
                h = g * HG + hh
                kn, k, k_ready = ks.pop(0)
                for qt in range(QT):
                    n = hh * QT + qt
                    if l == 0:
                        for c in range(-(-NK // BANK)):
                            a, w = c * BANK, min(BANK, NK - c * BANK)
                            si, ps, free = self.ring["score"].take()
                            t0 = p.op("pe", lambda e: e.matmul(ps[:, 0:w], q[0:ROWS, hh, qt * P:(qt + 1) * P],
                                                               k[0:ROWS, a:a + w], start=True, stop=True),
                                      [q_ready, k_ready, free], w / 2400)
                            last = p.op("dve", lambda e: e.tensor_reduce(z["part"][:, n, c:c + 1], ps[:, 0:w], AX.X,
                                                                         ALU.max), [t0, read], w / 900, alone=True)
                            self.ring["score"].release(si, last)
                            yield step / 4, self.ring["score"].next_free()
                    else:
                        bi, s, sfree = self.ring["s"].take()
                        for c in range(-(-NK // (2 * BANK))):
                            a, w = c * 2 * BANK, min(2 * BANK, NK - c * 2 * BANK)
                            si, ps, free = self.ring["wide"].take()

                            def mm(e):
                                for b in range(0, w, BANK):
                                    r = e.matmul(ps[:, b:min(b + BANK, w)], q[0:ROWS, hh, qt * P:(qt + 1) * P],
                                                 k[0:ROWS, a + b:a + min(b + BANK, w)], start=True, stop=True)
                                return r
                            t0 = p.op("pe", mm, [q_ready, k_ready, free], w / 2400)
                            last = p.op("act", lambda e: e.activation(s[:, a:a + w], ps[:, 0:w], ACT.Copy), [t0, sfree],
                                        0.2 + w / 1000)
                            self.ring["wide"].release(si, last)
                            yield step / 8
                        yield from rank(step * 3 / 4)
                        late.append(dict(s=s, buf=bi, n=n, g=g, ready=last, flag=None))
                kring.release(kn, t0)
                if h + 2 < H:
                    ks.append(load_k(h + 2))
            qring.release(qn, t0)
            if l == 0:
                last = p.op("dve", lambda e: e.tensor_reduce(z["mx"][:, :], z["part"][:, :, :], AX.X, ALU.max),
                            [last, z["src_free"]])
                read = last
                yield step / 4, last
                self.shift_rows(z, z["mx"], i, g, d.rows[l], last, name + "_rows")
        while late:
            yield from rank(step)

    def candidates(self, z, s, ready, span):
        p, m = self.p, self.m
        for half in (range(0, KC // 2), range(KC // 2, KC)):
            def f(e):
                for c in half:
                    r = e.max(m.cand[:, c, :], s[:, KCUT[c]:KCUT[c + 1]])
                return r
            p.op("dve", f, [ready, z["read"]], 1.8, alone=True)
            yield span

    def kth(self, z, tile, span):
        p, m, n = self.p, self.m, tile["n"]
        flat_cand, left = (x[:, :, :].rearrange("p c k -> p (c k)") for x in (m.cand, m.left))
        out = [z["ends"][:, n, 0, :], m.top[:, 0, :], m.top[:, 1, :], z["ends"][:, n, 1, :]]
        p.op("dve", lambda e: e.max(out[0], flat_cand))
        for r in range(1, TOPK // 8):
            p.op("dve", lambda e: e.match_replace(left, out[r - 1], flat_cand if r == 1 else left, NEG))
            p.op("dve", lambda e: e.max(out[r], left))
        yield span
        p.op("dve", lambda e: e.tensor_reduce(z["eighth"][:, :], m.cand[:, :, 7], AX.X, ALU.max))
        tile["flag"] = p.op("dve", lambda e: e.tensor_tensor(z["flag"][:, :], z["eighth"][:, :], out[-1][:, 7:8], ALU.is_gt))

    def check(self, z, tile):
        p, m, s, n = self.p, self.m, tile["s"], tile["n"]
        i, ps, free = self.ring["small"].take()
        t = p.op("pe", lambda e: e.matmul(ps[0:1, 0:1], z["flag"][:, :], m.ones_col[:, :], start=True, stop=True),
                 [tile["flag"], free])
        t = p.op("dve", lambda e: e.tensor_copy(z["many"][:, :], ps[0:1, 0:1]), [t])
        self.ring["small"].release(i, t)
        p.wait("dve", [("dve", p.count["dve"], p.sem["dve"])])
        e = p.eng["dve"]
        e.reg_load(m.many_reg, z["many"][0:1, 0:1])
        with e.If(e.snap(m.many_reg, min_val=0, max_val=P) > 0):
            out = [z["ends"][:, n, 0, :], m.top[:, 0, :], m.top[:, 1, :], z["ends"][:, n, 1, :]]
            e.sem_clear(m.redo)
            steps = 0
            for r in range(TOPK // 8):
                if r:
                    e.match_replace(s[:, :], out[r - 1], s[:, :], NEG).then_inc(m.redo, 1)
                    steps += 1
                    e.wait_ge(m.redo, steps)
                e.max(out[r], s[:, :]).then_inc(m.redo, 1)
                steps += 1
                e.wait_ge(m.redo, steps)
        return p.op("dve", lambda e: e.nop(nofuse=True))

    def threshold(self, z):
        p = self.p
        def stt(out, x, c, y, op):
            return lambda e: e.scalar_tensor_tensor(out, x, c, y, ALU.mult, op)
        greatest, kth = z["ends"][:, :, 0, 0], z["ends"][:, :, 1, 7]
        t = p.op("dve", stt(z["th"][:, :], greatest, -1.0, greatest, ALU.max), [z["src_free"]])
        t = p.op("dve", stt(z["th"][:, :], z["th"][:, :], -ROUND, kth, ALU.add), [t])
        t = p.op("dve", stt(z["size"][:, :], kth, -1.0, kth, ALU.max), [t])
        t = p.op("dve", stt(z["th"][:, :], z["size"][:, :], -ROUND, z["th"][:, :], ALU.add), [t])
        return p.op("dve", lambda e: e.scalar_tensor_tensor(z["th"][:, :], greatest, -GUARD, z["th"][:, :],
                                                            ALU.add, ALU.max), [t])

    def weigh(self, g, nk, kq, v, topk, step, last_group, z):
        p, m = self.p, self.m
        pend = []
        while not self.ring["att"].ready(1):
            yield 0.25
        ai, ap, afree = self.ring["att"].take()

        def sums():
            c, kc, pi, pr, t2 = pend.pop(0)

            def mm(e):
                for j in range(HG):
                    r = e.matmul(ap[32 * j:32 * j + HD + 1, 0:S], v[0:kc, c, g * HG + j, :],
                                 pr[0:kc, j * S:(j + 1) * S], start=(c == 0), stop=(c * P + kc == nk),
                                 tile_position=(0, 32 * j), skip_group_check=True)
                return r
            t3 = p.op("pe", mm, [t2, afree if c == 0 else None], 1.75)
            self.ring["prob"].release(pi, t3)
            return t3
        def scores(c):
            kc = chunk(nk, c)
            k, q, c0, ready, done = kq(c)
            i, ps, free = self.ring["wide"].take()

            def mm(e):
                for j in range(HG):
                    r = e.matmul(ps[0:kc, j * S:(j + 1) * S], k[0:ROWX, j, c0:c0 + kc], q[0:ROWX, j, :],
                                 start=(j % 2 == 0), stop=not topk, skip_group_check=True)
                return r
            t = p.op("pe", mm, [ready, free], 0.44)
            done(t)
            if topk:
                ci, cut, cfree = self.ring["below"].take()
                t = p.op("act", lambda e: e.activation(cut[0:kc, :], ps[0:kc, :], ACT.Relu, scale=-STEEP), [t, cfree], 1.1)
                return c, kc, i, ps, t, ci, cut
            return c, kc, i, ps, t, None, None

        def weights(c, kc, i, ps, t, ci, cut):
            if topk:
                def mm(e):
                    for b in range(0, HG * S, BANK):
                        r = e.matmul(ps[0:kc, b:b + BANK], m.minus_ident[0:kc, 0:kc], cut[0:kc, b:b + BANK],
                                     start=False, stop=True, skip_group_check=True)
                    return r
                t = p.op("pe", mm, [t], 0.43)
                self.ring["below"].release(ci, t)
            pi, pr, pfree = self.ring["prob"].take()
            t = p.op("act", lambda e: e.activation(pr[0:kc, :], ps[0:kc, :], ACT.Exp, scale=SCALE), [t, pfree], 1.1)
            self.ring["wide"].release(i, t)
            pend.append((c, kc, pi, pr, t))
        chunks, lot = list(range(-(-nk // P))), 2 if topk else 1
        for c in range(0, len(chunks), lot):
            made = [scores(cc) for cc in chunks[c:c + lot]]
            while pend:
                sums()
            for x in made:
                weights(*x)
            yield step * lot
        while len(pend) > 1:
            sums()
        last = sums()
        t0 = p.op("act", lambda e: e.activation(z["u"][:, :], ap[:, 0:S], ACT.Copy), [last, z["u_free"]], 0.45)
        self.ring["att"].release(ai, t0)
        yield 0.2, t0
        i, ps, free = self.ring["small"].take()

        def tr(e):
            for t in range(QT):
                r = e.transpose(ps[:, t * P:(t + 1) * P], z["u"][:, t * P:(t + 1) * P], m.ident[:, :])
            return r
        t1 = p.op("pe", tr, [t0, free])
        z["u_free"] = t1
        pv = ps[:, 0:QT * P].rearrange("p (t j r) -> p t j r", t=QT, j=HG)
        t2 = p.op("dve", lambda e: e.reciprocal(z["rec"][:, :, :], pv[:, :, :, HD]), [t1])

        def mul(e):
            for t in range(QT):
                o = z["o"][:, t, g * HG * HD:(g + 1) * HG * HD].rearrange("p (j r) -> p j r", j=HG)
                r = e.tensor_tensor(o, pv[:, t, :, 0:HD], z["rec"][:, t, :].unsqueeze(2).to_broadcast([P, HG, HD]),
                                    ALU.mult)
            return r
        z["o_ready"] = p.op("dve", mul, [t2])
        self.ring["small"].release(i, z["o_ready"])

    def stage_attend(self, l, i, step):
        p, m, d, z = self.p, self.m, self.d, self.m.z["att%d" % l]
        z["u_free"] = None
        name = "att%d" % l
        xs, xd = (d.x[i, :, :].rearrange("(t p) d -> p t d", p=P), d.x0[i]) if l == 0 else (d.x1[i], d.x2[i])
        kring, qring = self.ring["k_" + name], self.ring["q_" + name]
        KB = 4

        def load_q(g):
            n, q, free = qring.take()
            t = p.dma(f"q_{name}_{n}", [
                (q[0:ROWS, :, :], d.q_stack[l][i, :, :, g * HG:(g + 1) * HG, :].rearrange("n j h s -> (n j) h s")),
                (q[ROWS:ROWX, :, :].rearrange("k h s -> k (h s)"), d.rows[l][i, :, g, :, :].rearrange("k a s -> k (a s)"))],
                [free])
            return n, q, t

        def load_k(g, b):
            n, k, free = kring.take()
            a, w = b * KB * P, min(KB * P, NK - b * KB * P)
            t = p.dma(f"k_{name}_{n}", [(k[0:ROWS, :, 0:w], d.k_stack[l][i, :, :, g * HG:(g + 1) * HG, a:a + w]
                                         .rearrange("n j h s -> (n j) h s"))], [free])
            return n, k, t
        blocks = [(g, b) for g in range(G) for b in range(-(-NC // KB))]
        qs = [load_q(0)]
        ks = [load_k(*blocks.pop(0))]
        v_ready = p.dma(name + "_v", [(m.v[l][:, :, :, :].rearrange("p c h j -> p c (h j)")[:, 0:NC - 1, :],
                                       d.v[l][i, :, 0:NC - 1, :]),
                                      (m.v[l][0:chunk(NK, NC - 1), NC - 1, :, :].rearrange("p h j -> p (h j)"),
                                       d.v[l][i, 0:chunk(NK, NC - 1), NC - 1, :])])
        yield 0.3
        ks.append(load_k(*blocks.pop(0)))
        yield 0.3, v_ready
        for g in range(G):
            if g + 1 < G:
                qs.append(load_q(g + 1))
            qn, q, q_ready = qs.pop(0)
            cur = {}

            def kq(c):
                if c % KB == 0:
                    cur["k"] = ks.pop(0)
                n, k, ready = cur["k"]

                def done(t):
                    if c % KB == KB - 1 or c == NC - 1:
                        kring.release(n, t)
                        if blocks:
                            ks.append(load_k(*blocks.pop(0)))
                    if c == NC - 1:
                        qring.release(qn, t)
                return k, q, c % KB * P, [ready, q_ready, v_ready], done
            yield from self.weigh(g, NK, kq, m.v[l], l == 1, step, g == G - 1, z)
            if g == 0:
                x_ready = p.dma(name + "_x", [(z["x"][:, :, :], xs)])
            yield step
        yield 0.2, z["o_ready"]
        t = self.turn(z["o"], z["oT"], z["o_ready"])
        yield 0.2, t
        n, ps, free = self.ring["small"].take()

        def mm(e):
            for q in range(QT):
                e.matmul(ps[:, q * D:(q + 1) * D], z["oT"][:, q * P:(q + 1) * P], m.w_oT[:, l, :], start=True, stop=False)
                r = e.matmul(ps[:, q * D:(q + 1) * D], m.ones[:, :], m.b_o[:, l, :], start=False, stop=True)
            return r
        t = p.op("pe", mm, [t, free])
        t = p.op("dve", lambda e: e.scalar_tensor_tensor(flat(z["x"]), ps[:, 0:QT * D], m.gates[:, l:l + 1], flat(z["x"]),
                                                         ALU.mult, ALU.add), [t, x_ready])
        self.ring["small"].release(n, t)
        p.dma(name + "_out", [(xd, z["x"][:, :, :])], [t])

    def route(self, z, w, bias, over_all):
        p, m = self.p, self.m
        i, ps, free = self.ring["small"].take()

        def mm(e):
            for t in range(QT):
                e.matmul(ps[:, t * E:(t + 1) * E], z["xnT"][:, t * P:(t + 1) * P], w[:, :], start=True, stop=False)
                r = e.matmul(ps[:, t * E:(t + 1) * E], m.ones[:, :], bias[:, :], start=False, stop=True)
            return r
        t = p.op("pe", mm, [z["xnT_ready"], free])
        t = p.op("dve", lambda e: e.tensor_copy(flat(z["s"]), ps[:, 0:QT * E]), [t])
        self.ring["small"].release(i, t)

        def best(e):
            for q in range(QT):
                r = e.max(z["best"][:, q, :], z["s"][:, q, :])
            return r
        t = p.op("dve", best, [t])

        def where(e):
            for q in range(QT):
                r = e.max_index(z["at"][:, q, :], z["best"][:, q, :], z["s"][:, q, :])
            return r
        t = p.op("dve", where, [t])
        t = p.op("dve", lambda e: e.tensor_copy(z["atf"][:, :, :], z["at"][:, :, :]), [t])
        t = p.op("dve", lambda e: e.tensor_scalar(z["neg"][:, :], z["best"][:, :, 0], -1.0, None, ALU.mult), [t])
        yield 0.2, t

        def ex(e):
            for q in range(QT):
                r = e.activation(z["e"][:, q, :], z["s"][:, q, :], ACT.Exp, bias=z["neg"][:, q:q + 1])
            return r
        t = p.op("act", ex, [t])
        yield 0.2, t

        def pick(k, dst):
            def f(e):
                for q in range(QT):
                    r = e.scalar_tensor_tensor(dst[:, q, :], m.iota8[:, :], z["atf"][:, q, k:k + 1], z["e"][:, q, :],
                                               ALU.is_equal, ALU.mult)
                return r
            return f
        p.op("dve", pick(0, z["w"]), [t])
        t = p.op("dve", pick(1, z["w2"]))
        t = p.op("dve", lambda e: e.tensor_tensor(z["w"][:, :, :], z["w"][:, :, :], z["w2"][:, :, :], ALU.add), [t])
        whole = z["e"] if over_all else z["w"]
        t = p.op("dve", lambda e: e.tensor_reduce(z["sum"][:, :], whole[:, :, :], AX.X, ALU.add), [t])
        t = p.op("dve", lambda e: e.reciprocal(z["sum"][:, :], z["sum"][:, :]), [t])

        def fin(e):
            for q in range(QT):
                r = e.tensor_scalar(z["w"][:, q, :], z["w"][:, q, :], z["sum"][:, q:q + 1], None, ALU.mult)
            return r
        z["w_ready"] = p.op("dve", fin, [t])

    def add_expert(self, z, n, y, first, after):
        def f(e):
            for q in range(QT):
                w = z["w"][:, q, n:n + 1]
                if first:
                    r = e.tensor_scalar(z["acc"][:, q, :], y(q), w, None, ALU.mult)
                else:
                    r = e.scalar_tensor_tensor(z["acc"][:, q, :], y(q), w, z["acc"][:, q, :], ALU.mult, ALU.add)
            return r
        return self.p.op("dve", f, after)

    def gated(self, z, gate, ready):
        return self.p.op("dve", lambda e: e.scalar_tensor_tensor(
            flat(z["x"]), flat(z["acc"]), self.m.gates[:, gate:gate + 1], flat(z["x"]), ALU.mult, ALU.add), [ready])

    def stage_v(self, i, step):
        p, m, d, z = self.p, self.m, self.d, self.m.z["v"]
        x = p.dma("v_x", [(z["x"][:, :, :], d.x0[i])])
        yield 0.2, x
        yield from self.norm(z, x)
        yield 0.2, z["xnT_ready"]
        yield from self.route(z, m.w_r, m.b_r, False)
        yield 1
        acc = None
        for e0 in range(0, E, 2):
            hs = []
            while not self.ring["hid"].ready(2):
                yield 0.25
            for x_ in (e0, e0 + 1):
                n, ps, free = self.ring["wide"].take()

                def mm(e):
                    for k in range(PT):
                        r = e.matmul(ps[:, k * S:(k + 1) * S], m.w_1[:, x_, k * P:(k + 1) * P], z["xnT"][:, :],
                                     start=True, stop=True)
                    return r
                t0 = p.op("pe", mm, [z["xnT_ready"], free], 1.75)
                hs.append((x_, n, ps, t0))
            hid = []
            for x_, n, ps, t0 in hs:
                hn, hb, hfree = self.ring["hid"].take()

                def gl(e):
                    for k in range(PT):
                        r = e.activation(hb[:, k, :], ps[:, k * S:(k + 1) * S], ACT.Gelu_apprx_tanh,
                                         bias=m.b_1[:, x_, k:k + 1])
                    return r
                t1 = p.op("act", gl, [t0, hfree], 2.5)
                self.ring["wide"].release(n, t1)
                hid.append((x_, hn, hb, t1))
            yield step / 2
            for x_, hn, hb, t1 in hid:
                yield 0.1, t1
                n, ps, free = self.ring["small"].take()

                def mm2(e):
                    for q in range(QT):
                        e.matmul(ps[:, q * D:(q + 1) * D], m.ones[:, :], m.b_2[:, x_ * D:(x_ + 1) * D], start=True, stop=False)
                        for k in range(PT):
                            r = e.matmul(ps[:, q * D:(q + 1) * D], hb[:, k, q * P:(q + 1) * P], m.w_2[:, x_, k, :],
                                         start=False, stop=(k == PT - 1))
                    return r
                t2 = p.op("pe", mm2, [t1, free], 2.0)
                self.ring["hid"].release(hn, t2)
                acc = self.add_expert(z, x_, lambda q: ps[:, q * D:(q + 1) * D], x_ == 0, [t2, z["w_ready"], acc])
                self.ring["small"].release(n, acc)
                yield step
        t = self.gated(z, 2, acc)
        p.dma("v_out", [(d.x1[i], z["x"][:, :, :])], [t])
        yield 1
        yield from self.norm(z, t)
        yield 0.2, z["xnT_ready"]
        self.to_stack(m.w_qT[:, 1, :], z["xnT"][:, :], m.b_q[:, 1:2], S, d.q_stack[1][i], QPART, slice(0, S), z["xnT_ready"])

    def stage_z(self, i, step):
        p, m, d, z = self.p, self.m, self.d, self.m.z["z"]
        z["u_free"] = z["sent"] = z["src_free"] = None
        x = p.dma("z_x", [(z["x"][:, :, :], d.x2[i])])
        yield 0.2, x
        yield from self.norm(z, x)
        yield 0.2, z["xnT_ready"]
        sent = [self.to_stack(m.w_qkv[:, n, :], z["xnT"][:, :], m.b_qk[:, n:n + 1], S, d.self_stack[n][i],
                              (QPART, KPART)[n], slice(0, S), z["xnT_ready"]) for n in range(2)]
        n, ps, free = self.ring["small"].take()

        def mm(e):
            for q in range(QT):
                e.matmul(ps[:, q * D:(q + 1) * D], z["xnT"][:, q * P:(q + 1) * P], m.w_qkv[:, 2, :], start=True, stop=False)
                r = e.matmul(ps[:, q * D:(q + 1) * D], m.ones[:, :], m.b_v2[:, :], start=False, stop=True)
            return r
        t = p.op("pe", mm, [z["xnT_ready"], free])
        v_ready = p.op("act", lambda e: e.activation(m.v[2][:, :, :, 0:HD].rearrange("p t h j -> p (t h) j"),
                                                     ps[:, 0:QT * D].rearrange("p (c j) -> p c j", j=HD), ACT.Copy), [t])
        self.ring["small"].release(n, v_ready)
        yield 1
        yield from self.route(z, m.w_g, m.b_g, True)
        yield 1
        acc = None
        for q in range(QT):
            while not self.ring["hid"].ready(1):
                yield 0.25
            n, ps, free = self.ring["wide"].take()

            def mm3(e):
                for b in range(0, E * D, BANK):
                    e.matmul(ps[:, b:b + BANK], z["xnT"][:, q * P:(q + 1) * P], m.w_e[:, b:b + BANK], start=True, stop=False)
                    r = e.matmul(ps[:, b:b + BANK], m.ones_e[:, :], m.b_e[:, b:b + BANK], start=False, stop=True)
                return r
            t = p.op("pe", mm3, [z["xnT_ready"], free], 3.5)
            yi, y, yfree = self.ring["hid"].take()
            t = p.op("act", lambda e: e.activation(y[:, :, :].rearrange("p a b -> p (a b)"), ps[:, :], ACT.Copy), [t, yfree])
            self.ring["wide"].release(n, t)
            yf = y[:, :, :].rearrange("p a b -> p (a b)")
            for n in range(E):
                w = z["w"][:, q, n:n + 1]
                yn = yf[:, n * D:(n + 1) * D]
                if n == 0:
                    t = p.op("dve", lambda e: e.tensor_scalar(z["acc"][:, q, :], yn, w, None, ALU.mult), [t, z["w_ready"]])
                else:
                    t = p.op("dve", lambda e: e.scalar_tensor_tensor(z["acc"][:, q, :], yn, w, z["acc"][:, q, :], ALU.mult,
                                                                     ALU.add), [t])
            self.ring["hid"].release(yi, t)
            acc = t
            yield step
        for g in range(G):
            hs = slice(g * HG, (g + 1) * HG)
            n, (kt, qt_), free = self.ring["kq_self"].take()
            t0 = p.dma(f"kq_self{n}", [(kt[0:ROWS, :, :], d.self_stack[1][i, :, :, hs, :].rearrange("n j h s -> (n j) h s")),
                                       (qt_[0:ROWS, :, :], d.self_stack[0][i, :, :, hs, :].rearrange("n j h s -> (n j) h s"))],
                       [sent, free])
            yield 0.2, t0
            for h in range(HG):
                si, ps, sfree = self.ring["score"].take()

                def mm4(e):
                    for q in range(QT):
                        r = e.matmul(ps[:, q * S:(q + 1) * S], qt_[0:ROWS, h, q * P:(q + 1) * P], kt[0:ROWS, h, :],
                                     start=True, stop=True)
                    return r
                t1 = p.op("pe", mm4, [t0, sfree])
                t2 = p.op("dve", lambda e: e.tensor_reduce(z["mx"][:, h * QT:(h + 1) * QT],
                                                           ps[:, :].rearrange("p (q s) -> p q s", q=QT), AX.X, ALU.max),
                          [t1, z["src_free"]])
                self.ring["score"].release(si, t2)
                yield step / 2, t2
            t3 = self.shift_rows(z, z["mx"], i, g, d.rows[2], t2, "z_rows")
            t4 = p.dma(f"z_rows_in{n}", [(qt_[ROWS:ROWX, :, :].rearrange("k h s -> k (h s)"),
                                          d.rows[2][i, :, g, :, :].rearrange("k a s -> k (a s)"))], [t3])
            yield 0.2, t4

            def kq(c):
                def done(t):
                    if c == QT - 1:
                        self.ring["kq_self"].release(n, t)
                return kt, qt_, c * P, [t4, v_ready], done
            yield from self.weigh(g, S, kq, m.v[2], False, 0.4, g == G - 1, z)
            yield 1
        t = p.op("dve", lambda e: e.tensor_tensor(flat(z["acc"]), flat(z["acc"]), flat(z["o"]), ALU.add), [acc, z["o_ready"]])
        t = self.gated(z, 3, t)
        p.dma("z_out", [(d.out[i, :, :].rearrange("(t p) d -> p t d", p=P), z["x"][:, :, :])], [t])


def flat(x):
    return x[:, :, :].rearrange("p t d -> p (t d)")


class Buffers:
    pass


class Dram:
    pass


def build(nc, a, out):
    ctx = ExitStack()
    with ctx, nc.allow_non_contiguous_dma(reason="small strided parts of weights and biases"):
        def sb(name, shape, dt=F32):
            return ctx.enter_context(nc.sbuf_tensor(name, shape, dt))

        def psum(name, n):
            return ctx.enter_context(nc.psum_tensor(name, [P, n], F32))
        m, d = Buffers(), Dram()
        m.ident, m.ones_rows = sb("ident", [P, P]), sb("ones_rows", [33, P])
        m.ones, m.ones_e = m.ones_rows[0:1, :], m.ones_rows[32:33, :]
        m.minus_ident = sb("minus_ident", [P, P], BF16)
        m.ones_col = sb("ones_col", [P, 1])
        m.iota8, m.half = sb("iota8", [P, E]), sb("half", [P, QT])
        m.gates = sb("gates", [P, 4])
        m.w_kT, m.w_qT, m.w_vT, m.w_oT = (sb(n, [P, 2, D]) for n in ("w_kT", "w_qT", "w_vT", "w_oT"))
        m.b_q, m.b_k, m.b_v, m.b_o = sb("b_q", [P, 2]), sb("b_k", [P, 2]), sb("b_v", [P, 2]), sb("b_o", [1, 2, D])
        m.w_1, m.b_1 = sb("w_1", [P, E, FF]), sb("b_1", [P, E, PT])
        m.w_2, m.b_rows = sb("w_2", [P, E, PT, D]), sb("b_rows", [33, E * D])
        m.b_2, m.b_e = m.b_rows[0:1, :], m.b_rows[32:33, :]
        m.w_r, m.b_r, m.w_g, m.b_g = sb("w_r", [P, E]), sb("b_r", [1, E]), sb("w_g", [P, E]), sb("b_g", [1, E])
        m.w_qkv, m.b_qk, m.b_v2 = sb("w_qkv", [P, 3, D]), sb("b_qk", [P, 2]), sb("b_v2", [1, D])
        m.w_e = sb("w_e", [P, E * D])

        def dram(name, shape, dt=F32):
            return nc.dram_tensor(name, shape, dt).ap()
        d.x, d.ctx, d.out = a["x"], a["ctx_1024"], out
        d.k_stack = [dram(f"k_stack{l}", (B, NT, HD, H, NK), BF16) for l in range(2)]
        d.q_stack = [dram(f"q_stack{l}", (B, NT, HD, H, S), BF16) for l in range(2)]
        d.self_stack = [dram(f"self_stack{n}", (B, NT, HD, H, S), BF16) for n in range(2)]
        d.rows = [dram(f"rows{l}", (B, 3, G, HG * QT, P), BF16) for l in range(3)]
        d.v = [dram(f"v_dram{l}", (B, P, NC, H * (HD + 1))) for l in range(2)]
        d.x0, d.x1, d.x2 = (dram(n, (B, P, QT, D)) for n in ("x0", "x1", "x2"))

        m.ctxT = sb("ctxT", [P, NK])
        m.v = [sb("v0", [P, NC, H, HD + 1]), sb("v1", [P, NC, H, HD + 1]), sb("v2", [P, QT, H, HD + 1])]
        m.cand, m.left, m.top = sb("cand", [P, KC, 8]), sb("left", [P, KC, 8]), sb("top", [P, TOPK // 8 - 2, 8])
        m.rings = {
            "wide": [psum(f"wide{n}", 2 * BANK) for n in range(2)],
            "score": [psum(f"score{n}", BANK) for n in range(2)],
            "att": [psum("att", BANK)],
            "small": [psum("small", BANK)],
            "split": [(sb(f"split_f{n}", [P, BANK]), sb(f"split_b{n}", [P, 3, BANK], BF16)) for n in range(2)],
            "v_out": [sb(f"v_out{n}", [P, 4 * H, HD + 1]) for n in range(2)],
            "s": [sb(f"s{n}", [P, NK]) for n in range(3)],
            "below": [sb(f"below{n}", [P, HG * S], BF16) for n in range(2)],
            "prob": [sb(f"prob{n}", [P, HG * S]) for n in range(3)],
            "hid": [sb(f"hid{n}", [P, PT, S]) for n in range(2)],
            "kq_self": [(sb(f"k_self{n}", [64, HG, S], BF16), sb(f"q_self{n}", [64, HG, S], BF16)) for n in range(1)],
        }
        for l in range(2):
            m.rings[f"k_scan{l}"] = [sb(f"k_scan{l}_{n}", [ROWS, NK], BF16) for n in range(2)]
            m.rings[f"q_scan{l}"] = [sb(f"q_scan{l}_{n}", [ROWS, HG, S], BF16) for n in range(2)]
            m.rings[f"k_att{l}"] = [sb(f"k_att{l}_{n}", [64, HG, 4 * P], BF16) for n in range(2)]
            m.rings[f"q_att{l}"] = [sb(f"q_att{l}_{n}", [64, HG, S], BF16) for n in range(2)]
        m.z = {}

        def state(name, **shapes):
            m.z[name] = {k: sb(f"{name}_{k}", shape, dt) for k, (shape, dt) in shapes.items()}
        NORM = dict(x=([P, QT, D], F32), xn=([P, QT, D], F32), xnT=([P, S], F32), stats=([P, QT, 6], F32),
                    mv=([P, QT, 2], F32), rstd=([P, QT], F32))
        SHIFT = dict(mx=([P, HG * QT], F32), minus=([8, P], F32), res=([8, P], F32), shift=([8, 3, P], BF16))
        SUM = dict(u=([P, S], F32), rec=([P, QT, HG], F32), o=([P, QT, D], F32))
        ROUTE = dict(s=([P, QT, E], F32), best=([P, QT, 8], F32), at=([P, QT, 8], U32), atf=([P, QT, 8], F32),
                     e=([P, QT, E], F32), w=([P, QT, E], F32), w2=([P, QT, E], F32), sum=([P, QT], F32),
                     acc=([P, QT, D], F32))
        state("w", **NORM)
        state("scan0", part=([P, HG * QT, 4], F32), **SHIFT)
        state("scan1", ends=([P, HG * QT, 2, 8], F32), size=([P, HG * QT], F32), th=([P, HG * QT], F32),
              eighth=([P, 1], F32), flag=([P, 1], F32), many=([1, 1], I32), **SHIFT)
        for l in range(2):
            state(f"att{l}", x=([P, QT, D], F32), oT=([P, S], F32), **SUM)
        state("v", neg=([P, QT], F32), **NORM, **ROUTE)
        state("z", neg=([P, QT], F32), **NORM, **SHIFT, **SUM, **ROUTE)
        sems = {k: ctx.enter_context(nc.semaphore(f"{k}_done")) for k in ("pe", "act", "dve", "pool")}
        dma_sems = [ctx.enter_context(nc.semaphore(f"dma_done{n}")) for n in range(48)]
        m.redo = ctx.enter_context(nc.semaphore("redo"))
        m.many_reg = nc.vector.alloc_register("many_reg")
        nums = [s.num for s in list(sems.values()) + dma_sems]
        assert max(nums) - min(nums) + 1 == len(nums)

        def end_pass(p):
            p.run()
            nc.all_engine_barrier(sems_to_clear=range(min(nums), max(nums) + 1))

        p = Pass(nc, sems, dma_sems)
        row = lambda name: a[name].rearrange("(o n) -> o n", o=1)
        col = lambda name: a[name].rearrange("(p o) -> p o", o=1)
        loads = []
        for l, pre in enumerate(("L0_xattn_", "L1_xattn_")):
            loads += [(m.w_kT[:, l, :], a[pre + "Wk"]), (m.w_qT[:, l, :], a[pre + "Wq"]),
                      (m.w_vT[:, l, :], a[pre + "Wv"]), (m.w_oT[:, l, :], a[pre + "Wo"]),
                      (m.b_q[:, l:l + 1], col(pre + "bq")), (m.b_k[:, l:l + 1], col(pre + "bk")),
                      (m.b_v[:, l:l + 1], col(pre + "bv")), (m.b_o[:, l, :], row(pre + "bo"))]
        loads += [(m.w_1[:, :, :], a["L0_ffn_W1"].rearrange("e d f -> d e f")),
                  (m.b_2[:, :], a["L0_ffn_b2"].rearrange("(o e) d -> o (e d)", o=1)),
                  (m.w_r[:, :], a["L0_ffn_Wr"]), (m.b_r[:, :], row("L0_ffn_br")),
                  (m.w_qkv[:, :, :], a["L1_ffn_W_qkv"].rearrange("d (n f) -> d n f", n=3)),
                  (m.b_v2[:, :], row("L1_ffn_b_qkv")[:, 2 * D:3 * D]),
                  (m.w_g[:, :], a["L1_ffn_W_gate"]), (m.b_g[:, :], row("L1_ffn_b_gate")),
                  (m.w_e[:, :].rearrange("p (e f) -> p e f", e=E), a["L1_ffn_W_experts"].rearrange("e d f -> d e f")),
                  (m.b_e[:, :], a["L1_ffn_b_experts"].rearrange("(o e) f -> o (e f)", o=1)),
                  (m.gates[:, 0:2], row("g_xattn").to_broadcast([P, 2])),
                  (m.gates[:, 2:4], row("g_ffn").to_broadcast([P, 2]))]
        loads += [(m.b_qk[:, n:n + 1], a["L1_ffn_b_qkv"][n * D:(n + 1) * D].rearrange("(p o) -> p o", o=1))
                  for n in range(2)]
        for e_ in range(E):
            loads += [(m.b_1[:, e_, :], a["L0_ffn_b1"][e_, :].rearrange("(t p) -> p t", p=P)),
                      (m.w_2[:, e_, :, :], a["L0_ffn_W2"][e_, :, :].rearrange("(t p) d -> p t d", p=P))]
        loaded = p.dma("weights", loads)
        t = p.op("pool", lambda e: e.memset(m.ident[:, :], 0.0))
        p.op("pool", lambda e: e.affine_select(out=m.ident[:, :], in_=m.ident[:, :], compare_op=ALU.not_equal,
                                               fill=1.0, base=0, pattern=[[-1, P]], channel_multiplier=1), [t])
        t = p.op("pool", lambda e: e.memset(m.minus_ident[:, :], 0.0))
        p.op("pool", lambda e: e.affine_select(out=m.minus_ident[:, :], in_=m.minus_ident[:, :],
                                               compare_op=ALU.not_equal, fill=-1.0, base=0, pattern=[[-1, P]],
                                               channel_multiplier=1), [t])
        for j in range(E):
            p.op("pool", lambda e: e.memset(m.iota8[:, j:j + 1], float(j)))
        p.op("pool", lambda e: e.memset(m.half[:, :], -0.5))
        p.op("pool", lambda e: e.memset(m.ones_rows[:, :], 1.0))
        p.op("pool", lambda e: e.memset(m.ones_col[:, :], 1.0))
        for buf in (*m.rings["k_att0"], *m.rings["k_att1"], m.rings["kq_self"][0][0]):
            p.op("pool", lambda e: e.memset(buf[:, :, :], 1.0))
        for buf in (*m.rings["v_out"],):
            p.op("pool", lambda e: e.memset(buf[:, :, :], 1.0))
        p.op("pool", lambda e: e.memset(m.v[2][:, :, :, :], 1.0))
        att, u = m.rings["att"][0], m.z["z"]["u"]
        t = p.op("dve", lambda e: e.memset(u[:, :], 0.0))
        p.op("pe", lambda e: e.matmul(att[:, 0:S], u[:, 0:P], u[:, :], start=True, stop=True), [t])
        p.op("act", lambda e: e.activation(m.gates[:, :], m.gates[:, :], ACT.Tanh), [loaded])
        small = m.rings["small"][0]
        for l in range(2):
            t = p.op("pe", lambda e: e.matmul(small[0:1, l * D:(l + 1) * D], m.b_v[:, l:l + 1], m.w_oT[:, l, :],
                                              start=True, stop=True), [loaded, t if l else None])
            t = p.op("dve", lambda e: e.tensor_tensor(m.b_o[:, l, :], small[0:1, l * D:(l + 1) * D], m.b_o[:, l, :],
                                                      ALU.add), [t])
        end_pass(p)

        AFTER = dict(w=0, scan0=1, att0=2, v=3, scan1=4, att1=5, z=6)
        DEPTH = max(AFTER.values())

        def one_pass(n, active):
            p = Pass(nc, sems, dma_sems)
            s = Stages(p, m, d)
            make = dict(w=lambda i: (0.1, s.stage_w(i)), scan0=lambda i: (0.05, s.stage_scan(0, i, SCAN0)),
                        att0=lambda i: (ATT0_AT, s.stage_attend(0, i, ATT0)), v=lambda i: (V_AT, s.stage_v(i, V_STEP)),
                        scan1=lambda i: (0.0, s.stage_scan(1, i, SCAN1)),
                        att1=lambda i: (0.2, s.stage_attend(1, i, ATT1)),
                        z=lambda i: (Z_AT, s.stage_z(i, Z_STEP)))
            for name, k in AFTER.items():
                if name in active:
                    p.stage(*make[name](n - k))
            end_pass(p)
        for n in range(DEPTH):
            one_pass(n, [k for k, v in AFTER.items() if n >= v])
        with nc.Fori(DEPTH, B) as n:
            one_pass(n, list(AFTER))
        for n in range(B, B + DEPTH):
            one_pass(n, [k for k, v in AFTER.items() if n - v < B])


_OUTS = [((B, S, D), "float32")]


def kernel(**inputs):
    import numpy as _np
    import concourse.bacc as _bacc
    from concourse import mybir as _mybir
    from concourse.bass_utils import run_bass_kernel_spmd as _run

    nc = _bacc.Bacc("TRN2", target_bir_lowering=False, num_devices=1)
    arrays, args = {}, {}
    for name in inputs:
        v = _np.asarray(inputs[name])
        if name == "ctx_1024":
            v = v.transpose(0, 2, 1)
        elif name.split("_")[-1] in ("Wq", "Wk", "Wv", "Wo"):
            v = v.T
        v = _np.ascontiguousarray(v)
        arrays[f"in_{name}_dram"] = v
        args[name] = nc.dram_tensor(f"in_{name}_dram", v.shape, _mybir.dt.from_np(v.dtype), kind="ExternalInput").ap()
    outs = [nc.dram_tensor(f"out_{i}_dram", shape, _mybir.dt.from_np(_np.dtype(dtype)), kind="ExternalOutput").ap()
            for i, (shape, dtype) in enumerate(_OUTS)]
    build(nc, args, outs[0])
    r = _run(nc, [arrays], core_ids=[0])
    return r.results[0]["out_0_dram"]
```
